# Optimizing a Trainium2 kernel written in Bass

```python
import numpy as np
import jax
import jax.numpy as jnp

def _softmax(x, axis=-1):
    return jax.nn.softmax(x, axis=axis)

def _gelu(x):
    return jax.nn.gelu(x, approximate=True)

def _silu(x):
    return jax.nn.silu(x)

def _sigmoid(x):
    return jax.nn.sigmoid(x)

def _layernorm(x, axis=-1, eps=1e-05):
    m = jnp.mean(x, axis=axis, keepdims=True)
    v = jnp.var(x, axis=axis, keepdims=True)
    return (x - m) / jnp.sqrt(v + eps)

def _scatter_add(tgt, idx, src, axis=0):
    return tgt.at[idx].add(src)

def _segment_sum(src, seg, n):
    return jax.ops.segment_sum(src, seg, n)
kernel_name = 'mk_vit_tower_postln_d1_tok_img1024_r4_a9155d'

def setup_inputs(seed: int=0):
    np.random.seed(seed)
    _w = jnp.asarray

    def _rec_inputs():
        import jax
        import jax.numpy as jnp
        _rk = jax.random.key(seed)
        x = -0.000222058 + 0.999998 * jax.random.normal(jax.random.fold_in(_rk, 1), (64, 3, 64, 64), jnp.float32)
        return x
    x = _rec_inputs()

    def _L0_tok_setup():
        import jax, jax.numpy as jnp
        import numpy as np
        IMG, PS, C, OUT = (64, 16, 3, 256)
        NP = IMG // PS
        IN_FEAT = C * PS * PS
        key = jax.random.key(seed)
        k1, k2, k3, k4 = jax.random.split(key, 4)
        x = jax.random.normal(k1, (128, C, IMG, IMG), dtype=jnp.float32)
        W = jax.random.normal(k2, (OUT, IN_FEAT), dtype=jnp.float32) / np.sqrt(IN_FEAT)
        b = jax.random.normal(k3, (OUT,), dtype=jnp.float32) * 0.01
        pos_emb = jax.random.normal(k4, (NP * NP, OUT), dtype=jnp.float32)
        return {'x': x, 'W': W, 'b': b, 'pos_emb': pos_emb}
    _L0_tok_all = _L0_tok_setup()
    _L0_tok_in = {k: v for k, v in _L0_tok_all.items() if k in ('W', 'b', 'pos_emb')}
    del _L0_tok_all

    def _L0_attn_setup():
        import jax, jax.numpy as jnp
        import numpy as np
        B, S, D = (4, 512, 256)
        key = jax.random.key(seed)
        k1, k2 = jax.random.split(key)
        x = jax.random.normal(k1, (B, S, D), dtype=jnp.float32)
        W = jax.random.normal(k2, (2 * D, D), dtype=jnp.float32) * 0.02
        return {'x': x, 'W': W}
    _L0_attn_all = _L0_attn_setup()
    _L0_attn_in = {k: v for k, v in _L0_attn_all.items() if k in ('W',)}
    del _L0_attn_all

    def _L0_ffn_setup():
        import jax, jax.numpy as jnp
        import numpy as np
        NUM_KEYS = 128
        TOP_K = 8
        NUM_HEADS = 4
        key = jax.random.key(seed)
        ks = jax.random.split(key, 8)
        b, t, d = (1, 512, 256)
        inter = 512
        E, h, ret = (4096, NUM_HEADS, 64)
        s = 0.02
        return {'hidden_states': jax.random.normal(ks[0], (b, t, d), jnp.float32), 'w_queries': jax.random.normal(ks[1], (h * ret, d), jnp.float32) * s, 'keys': jax.random.normal(ks[2], (h, NUM_KEYS, 2, ret // 2), jnp.float32) * s, 'down_embed': jax.random.normal(ks[3], (E, d), jnp.float32) * s, 'up_embed': jax.random.normal(ks[4], (E, d), jnp.float32) * s, 'w_gate': jax.random.normal(ks[5], (inter, d), jnp.float32) * s, 'w_up': jax.random.normal(ks[6], (inter, d), jnp.float32) * s, 'w_down': jax.random.normal(ks[7], (d, inter), jnp.float32) * s}
    _L0_ffn_all = _L0_ffn_setup()
    _L0_ffn_in = {k: v for k, v in _L0_ffn_all.items() if k in ('w_queries', 'keys', 'down_embed', 'up_embed', 'w_gate', 'w_up', 'w_down')}
    del _L0_ffn_all
    return {'x': x, 'L0_tok_W': _L0_tok_in['W'], 'L0_tok_b': _L0_tok_in['b'], 'L0_tok_pos_emb': _L0_tok_in['pos_emb'], 'L0_attn_W': _L0_attn_in['W'], 'L0_ffn_w_queries': _L0_ffn_in['w_queries'], 'L0_ffn_keys': _L0_ffn_in['keys'], 'L0_ffn_down_embed': _L0_ffn_in['down_embed'], 'L0_ffn_up_embed': _L0_ffn_in['up_embed'], 'L0_ffn_w_gate': _L0_ffn_in['w_gate'], 'L0_ffn_w_up': _L0_ffn_in['w_up'], 'L0_ffn_w_down': _L0_ffn_in['w_down']}

def reference(x, L0_tok_W, L0_tok_b, L0_tok_pos_emb, L0_attn_W, L0_ffn_w_queries, L0_ffn_keys, L0_ffn_down_embed, L0_ffn_up_embed, L0_ffn_w_gate, L0_ffn_w_up, L0_ffn_w_down):
    import jax
    import jax.numpy as jnp

    def _L0_tok_ref(x, W, b, pos_emb):
        import jax, jax.numpy as jnp
        import numpy as np
        IMG, PS, C, OUT = (64, 16, 3, 256)
        NP = IMG // PS
        IN_FEAT = C * PS * PS
        B = x.shape[0]
        p = x.reshape(B, C, NP, PS, NP, PS).transpose(0, 1, 2, 4, 3, 5)
        p = p.transpose(0, 2, 3, 1, 4, 5)
        p = p.reshape(B, NP * NP, IN_FEAT)
        out = jnp.einsum('bnf,of->bno', p, W) + b + pos_emb
        return out

    def _L0_attn_ref(x, W):
        import jax, jax.numpy as jnp
        import numpy as np
        B, S, D = (4, 512, 256)
        d = x.shape[-1]
        kv = x @ W.T
        K, V = (kv[..., :d], kv[..., d:])
        n = x.shape[-2]
        causal = jnp.tril(jnp.ones((n, n), dtype=bool))
        mask = jnp.where(causal, jnp.float32(0.0), -jnp.inf).astype(x.dtype)
        scores = jnp.einsum('bqd,bkd->bqk', x, K) + mask
        attn = jax.nn.softmax(scores, axis=-1)
        return x + jnp.einsum('bqk,bkd->bqd', attn, V)

    def _L0_ffn_ref(hidden_states, w_queries, keys, down_embed, up_embed, w_gate, w_up, w_down):
        import jax, jax.numpy as jnp
        import numpy as np
        NUM_KEYS = 128
        TOP_K = 8
        NUM_HEADS = 4
        b, t, d = hidden_states.shape
        h, nk, _, n = keys.shape
        k = TOP_K
        q = (hidden_states @ w_queries.T).reshape(b, t, 2, h, n)
        sim = jnp.einsum('btphn,hkpn->pbthk', q, keys)
        sx, ix = jax.lax.top_k(sim[0], k)
        sy, iy = jax.lax.top_k(sim[1], k)
        all_scores = (sx[..., :, None] + sy[..., None, :]).reshape(b, t, h, k * k)
        all_idx = (ix[..., :, None] * nk + iy[..., None, :]).reshape(b, t, h, k * k)
        scores, pos = jax.lax.top_k(all_scores, k)
        indices = jnp.take_along_axis(all_idx, pos, axis=-1)
        de = down_embed[indices]
        ue = up_embed[indices]
        ew = jnp.einsum('btd,bthkd->bthk', hidden_states, de)
        ew = jax.nn.silu(ew) * jax.nn.softmax(scores, axis=-1)
        experts_states = jnp.einsum('bthk,bthkd->btd', ew, ue)
        mlp = jax.nn.silu(hidden_states @ w_gate.T) * (hidden_states @ w_up.T) @ w_down.T
        return mlp + experts_states
    h = _L0_tok_ref(x, L0_tok_W, L0_tok_b, L0_tok_pos_emb)
    h = _layernorm(h + _L0_attn_ref(h, L0_attn_W), axis=-1)
    h = _layernorm(h + _L0_ffn_ref(h, L0_ffn_w_queries, L0_ffn_keys, L0_ffn_down_embed, L0_ffn_up_embed, L0_ffn_w_gate, L0_ffn_w_up, L0_ffn_w_down), axis=-1)
    return h

_drawn_inputs = setup_inputs


def setup_inputs(seed=0):
    import zlib

    import numpy as np

    out = dict(_drawn_inputs(seed))
    spreads = {}
    factors = {'L0_tok_b': 7.494,
     'L0_ffn_w_queries': 8.0,
     'L0_ffn_keys': 8.0,
     'L0_ffn_down_embed': 6.437,
     'L0_ffn_up_embed': 5.632}
    for name, (base, spread) in spreads.items():
        noise = np.random.default_rng([zlib.crc32(name.encode()), seed]).standard_normal(out[name].shape)
        drawn = base * np.exp(spread * noise) if base else spread * noise
        out[name] = jnp.asarray(drawn.astype(out[name].dtype))
    for name, factor in factors.items():
        out[name] = (out[name] * factor).astype(out[name].dtype)
    return out
```

```python
from contextlib import ExitStack

import concourse.bass as bass
from concourse import mybir

P = 128
IMAGES, CHANNELS, SIDE, PATCH = 64, 3, 64, 16
GRID = SIDE // PATCH
PATCHES = GRID * GRID
D = 256
DK = D // P
TOKENS = IMAGES * PATCHES
TILES = TOKENS // P
TILE_IMAGES = P // PATCHES
FEATURES = CHANNELS * PATCH * PATCH
FK = FEATURES // P
HALF = TOKENS // 2
HEADS, TOPK, KEYS = 4, 8, 128
PICKS = HEADS * TOPK
RET = 32
EXPERTS = 4096
CHUNKS = EXPERTS // P
INTER = 512
MK = INTER // P
EPS = 1e-5
WSCALE = float(2 ** 14)
CHUNKS_PER_TILE = CHUNKS // TILES
STEP = 16
HALF_TILES = 2 * TILES

ALU = mybir.AluOpType
ACT = mybir.ActivationFunctionType
AX_X = mybir.AxisListType.X
F32 = mybir.dt.float32
F16 = mybir.dt.float16
U32 = mybir.dt.uint32
ds = bass.ds


def vit_block_kernel(nc, x, tok_w, tok_b, pos_emb, attn_w, w_queries, keys, down_embed, up_embed,
                     w_gate, w_up, w_down, constants, out):
    with ExitStack() as ctx:
        def sb(name, shape, dt):
            return ctx.enter_context(nc.sbuf_tensor(name, shape, dt))

        def sem(name):
            return ctx.enter_context(nc.semaphore(name))

        S = sb("S", [P, CHUNKS, TOKENS], F32)
        S_flat = S[:, :, :].rearrange("p c t -> p (c t)")
        at = [0]

        def early(cols):
            at[0] += cols
            return S_flat[:, at[0] - cols:at[0]]

        x_rows = early(CHANNELS * 2 * PATCH * SIDE).rearrange("p (c l m) -> p c l m", c=CHANNELS, l=2)
        x_feats = early(CHANNELS * 2 * PATCH * SIDE).rearrange("p (c l w f) -> p c l w f", c=CHANNELS, l=2, w=GRID)
        xT = early(2 * FK * HALF).rearrange("p (l k t) -> p l k t", l=2, k=FK)
        tokw_nat = early(DK * FEATURES).rearrange("p (o f) -> p o f", o=DK)
        attnw_nat = early(2 * DK * D).rearrange("p (o f) -> p o f", f=D)
        queryw_nat = early(DK * D).rearrange("p (o f) -> p o f", f=D)
        gatew_nat = early(MK * D).rearrange("p (o f) -> p o f", f=D)
        upw_nat = early(MK * D).rearrange("p (o f) -> p o f", f=D)
        downw_nat = early(DK * INTER).rearrange("p (o f) -> p o f", f=INTER)
        keys_nat = early(2 * P).rearrange("p (s f) -> p s f", f=P)
        pos_nat = early(D)
        tokwT = early(FK * D).rearrange("p (k o) -> p k o", o=D)
        attnwT = early(DK * 2 * D).rearrange("p (k o) -> p k o", o=2 * D)
        h0T = early(DK * TOKENS).rearrange("p (k t) -> p k t", t=TOKENS)
        posT = early(DK * PATCHES).rearrange("p (k n) -> p k n", n=PATCHES)
        bias_rows = early(D)

        gatewT = sb("gatewT", [P, DK, INTER], F32)
        upwT = sb("upwT", [P, DK, INTER], F32)
        downwT = sb("downwT", [P, MK, D], F32)
        h1T = sb("h1T", [P, DK, TOKENS], F32)
        h1 = sb("h1", [P, TILES, D], F32)
        grid = sb("grid", [P, KEYS, STEP], F16)
        ident = sb("ident", [P, P], F32)
        slot_mask = sb("slot_mask", [P, 2], F32)
        iota8 = sb("iota8", [P, TOPK], F32)
        minus_half = sb("minus_half", [P, 1], F32)
        tab = sb("tab", [P, 4, D], F32)
        dT = sb("dT", [P, 2, DK, P], F32)
        selT = sb("selT", [P, TILES, 4, 32], F16)
        selW = sb("selW", [P, TILES, 2, 2, 32], F16)
        held = sb("held", [P, 1], F32)
        small = sb("small", [P, 64], F32)
        edge = sb("edge", [P, PICKS], F32)

        mT = sb("mT", [P, MK, TOKENS], F32)
        m_flat = mT[:, :, :].rearrange("p k t -> p (k t)")
        h0s = m_flat[:, 0:512].rearrange("p (u k t) -> p u k t", u=2, k=DK)
        kv = m_flat[:, 512:1536].rearrange("p (u f) -> p u f", u=2)
        h0x2 = m_flat[:, 1536:2048].rearrange("p (u f) -> p u f", u=2)
        masked = m_flat[:, 2048:2304].rearrange("p (u f) -> p u f", u=2)
        probs = m_flat[:, 2304:2560].rearrange("p (u f) -> p u f", u=2)
        probsT = m_flat[:, 2560:2816].rearrange("p (u f) -> p u f", u=2)
        y1 = m_flat[:, 2816:3328].rearrange("p (u f) -> p u f", u=2)
        h1s = m_flat[:, 3328:3840].rearrange("p (u f) -> p u f", u=2)
        mask = m_flat[:, 3840:3968]

        onehot_y = sb("onehot_y", [P, 2, KEYS, STEP], F16)
        r1 = onehot_y[:, :, :, :].rearrange("p u y s -> p (u y s)").bitcast(F32)
        keysB = r1[:, 0:1024].rearrange("p (s f) -> p s f", s=2)
        querywT = r1[:, 1024:1536].rearrange("p (k o) -> p k o", o=D)
        querywT_flat = r1[:, 1024:1536]
        qs = r1[:, 1536:1792].rearrange("p (s t) -> p s t", s=2)
        weighted_x = sb("weighted_x", [P, 2, 4, 32, STEP], F16)
        r2 = weighted_x[:, :, :, :, :].rearrange("p u q x s -> p (u q x s)").bitcast(F32)
        match = r2[:, 0:512].rearrange("p (a i) -> p a i", i=TOPK)
        picked = r2[:, 512:1024].rearrange("p (a i) -> p a i", i=TOPK)
        pair_sum = r2[:, 1024:1280]
        diffs = r2[:, 1280:1536].rearrange("p (t a) -> p t a", a=PICKS)
        exps = r2[:, 1536:1792].rearrange("p (t a) -> p t a", a=PICKS)
        onehot_x = sb("onehot_x", [P, 2, 32, STEP], F16)
        pack = onehot_x[:, :, :, :].rearrange("p u x s -> p (u x s)").rearrange(
            "p (t q a) -> p t q a", q=4, a=PICKS)

        top_val = sb("top_val", [P, 2, HEADS, TOPK], F32)
        top_idx = sb("top_idx", [P, 2, HEADS, TOPK], U32)
        pair_val = sb("pair_val", [P, HEADS, TOPK], F32)
        pair_pos = sb("pair_pos", [P, PICKS], U32)
        pair_ij = sb("pair_ij", [P, 2, PICKS], U32)
        row_xy = sb("row_xy", [P, 2, PICKS], F32)

        late = h1T[:, :, :].rearrange("p k t -> p (k t)")
        outT = late[:, 0:1024].rearrange("p (k t) -> p k t", k=DK)
        y2 = late[:, 1024:1536].rearrange("p (u f) -> p u f", u=2)
        result = late[:, 1536:2048].rearrange("p (u f) -> p u f", u=2)

        bank = [ctx.enter_context(nc.psum_tensor(f"bank{i}", [P, 512], F32)) for i in range(4)]
        region = [ctx.enter_context(nc.psum_tensor(f"region{i}", [P, 1024], F32)) for i in range(2)]
        turn = [region[0][:, 0:512], region[0][:, 512:1024], region[1][:, 0:512], region[1][:, 512:1024]]

        in_const = sem("in_const")
        in_tokw = sem("in_tokw")
        in_x = [[sem(f"in_x{l}{c}") for c in range(CHANNELS)] for l in range(2)]
        x_sorted = sem("x_sorted")
        in_attnw = sem("in_attnw")
        in_rest = sem("in_rest")
        in_tab = [sem(f"in_tab{j}") for j in range(4)]
        pool_ready = sem("pool_ready")
        turned = sem("turned")
        turned_by_act = sem("turned_by_act")
        turned_by_dve = sem("turned_by_dve")
        pos_biased = sem("pos_biased")
        pos_turned = sem("pos_turned")
        posT_ready = sem("posT_ready")
        keys_turned = sem("keys_turned")
        keysB_ready = sem("keysB_ready")
        embedded = sem("embedded")
        h0T_ready = sem("h0T_ready")
        h0s_ready = sem("h0s_ready")
        kv_done = sem("kv_done")
        kv_ready = sem("kv_ready")
        h0x2_ready = sem("h0x2_ready")
        scored = sem("scored")
        max_ready = sem("max_ready")
        probs_ready = sem("probs_ready")
        probs_turned = sem("probs_turned")
        probsT_ready = sem("probsT_ready")
        attended = sem("attended")
        var_ready = sem("var_ready")
        rstd_ready = sem("rstd_ready")
        h1s_ready = sem("h1s_ready")
        h1_ready = sem("h1_ready")
        h1_turned = sem("h1_turned")
        h1T_ready = sem("h1T_ready")
        query_done = sem("query_done")
        qs_ready = sem("qs_ready")
        sim_done = sem("sim_done")
        sims_read = sem("sims_read")
        tab_turned = sem("tab_turned")
        dT_ready = sem("dT_ready")
        dots_done = sem("dots_done")
        S_ready = sem("S_ready")
        diffs_ready = sem("diffs_ready")
        exps_ready = sem("exps_ready")
        gates_done = sem("gates_done")
        gate_ready = sem("gate_ready")
        hidden_free = sem("hidden_free")
        onehots_ready = sem("onehots_ready")
        region_done = sem("region_done")
        region_free = sem("region_free")
        chunk_used = sem("chunk_used")
        summed = sem("summed")
        outT_ready = sem("outT_ready")
        out_turned = sem("out_turned")
        var2_ready = sem("var2_ready")
        rstd2_ready = sem("rstd2_ready")
        result_ready = sem("result_ready")
        stored = [sem("stored0"), sem("stored1")]
        dve_step = sem("dve_step")

        block = ctx.enter_context(nc.Block())

        MEAN, VAR, VAR_EPS, RSTD, NEG_MAX, SUM, RECIP, STATS = range(8)

        def stat(u, n, cols=1):
            return small[:, 16 * u + n:16 * u + n + cols]

        def blocks_of(nat, rows, k):
            return [nat[:, o, k * P:(k + 1) * P] for o in range(rows)]

        def x_blocks(l, k):
            c, i = divmod(k, 2)
            return [x_feats[:, c, l, w, i * P:(i + 1) * P] for w in range(GRID)]

        def two(dst, k):
            return dst[:, k:k + 2, :].rearrange("p k o -> p (k o)")

        in_rest_all = 7 * 16
        groups = [("tokw", [b for k in (g, g + 1) for b in blocks_of(tokw_nat, DK, k)], two(tokwT, g), in_tokw, 16)
                  for g in range(0, FK, 2)]
        groups += [("x0", x_blocks(0, k), xT[:, 0, k, :], x_sorted, k // 2 + 1) for k in range(FK)]
        groups += [("x1", x_blocks(1, k), xT[:, 1, k, :], x_sorted, CHANNELS + k // 2 + 1) for k in range(FK)]
        groups += [("attnw", blocks_of(attnw_nat, 2 * DK, k), attnwT[:, k, :], in_attnw, 16) for k in range(DK)]
        groups += [("queryw", [b for k in range(DK) for b in blocks_of(queryw_nat, DK, k)], querywT_flat,
                    in_rest, in_rest_all)]
        groups += [("gatew", blocks_of(gatew_nat, MK, k), gatewT[:, k, :], in_rest, in_rest_all) for k in range(DK)]
        groups += [("upw", blocks_of(upw_nat, MK, k), upwT[:, k, :], in_rest, in_rest_all) for k in range(DK)]
        groups += [("downw", [b for k in (g, g + 1) for b in blocks_of(downw_nat, DK, k)], two(downwT, g),
                    in_rest, in_rest_all) for g in range(0, MK, 2)]
        names = [g[0] for g in groups]
        n_groups = len(groups)
        x1_starts, weights_start = names.index("x1"), names.index("attnw")

        def act_groups(g):
            return (g + 1) // 2

        sums = [[bank[2][:, :], bank[3][:, :]], [bank[0][:, :], bank[1][:, :]]]
        gate_out = dT[:, :, :, :].rearrange("p u k t -> p (u k t)")
        down_rows = down_embed.rearrange("(c p) d -> p c d", p=P)
        up_rows = up_embed.rearrange("(c p) d -> p c d", p=P)

        def out_slot(t):
            return [bank[2][:, 0:D], bank[3][:, 0:D], region[0][:, 0:D], region[0][:, 512:512 + D]][t % 4]

        @block.sync
        def _(sp):
            sp.dma_start(ident[:, :], constants[:, 0:P]).then_inc(in_const, 16)
            sp.dma_start(slot_mask[:, :], constants[:, 2 * P:2 * P + 2]).then_inc(in_const, 16)
            sp.dma_start(pos_nat[0:PATCHES, :], pos_emb).then_inc(in_const, 16)
            sp.dma_start(bias_rows[0:PATCHES, :], tok_b.partition_broadcast(PATCHES)).then_inc(in_const, 16)
            sp.dma_start(tokw_nat, tok_w.rearrange("(o p) f -> p o f", p=P)).then_inc(in_tokw, 16)
            image_rows = x.rearrange("b c (q l i) w -> q l b c i w", q=2, l=2, i=PATCH)
            for l in range(2):
                for c in range(CHANNELS):
                    for q in range(2):
                        sp.dma_start(x_rows[64 * q:64 * q + 64, c, l, :].rearrange("p (i w) -> p i w", w=SIDE),
                                     image_rows[q, l, :, c, :, :]).then_inc(in_x[l][c], 16)
            sp.dma_start(attnw_nat, attn_w.rearrange("(o p) f -> p o f", p=P)).then_inc(in_attnw, 16)
            sp.dma_start(queryw_nat, w_queries.rearrange("(o p) f -> p o f", p=P)).then_inc(in_rest, 16)
            sp.dma_start(gatew_nat, w_gate.rearrange("(o p) f -> p o f", p=P)).then_inc(in_rest, 16)
            sp.dma_start(upw_nat, w_up.rearrange("(o p) f -> p o f", p=P)).then_inc(in_rest, 16)
            sp.dma_start(downw_nat, w_down.rearrange("(o p) f -> p o f", p=P)).then_inc(in_rest, 16)
            for s in range(2):
                sp.dma_start(keys_nat[:, s, :].rearrange("p (h n) -> p h n", h=HEADS),
                             keys.rearrange("h k s n -> s k h n")[s]).then_inc(in_rest, 16)
            sp.dma_start(mask, constants[:, P:2 * P]).then_inc(in_rest, 16)
            for j in range(4):
                sp.dma_start(tab[:, j, :], down_rows[:, j, :]).then_inc(in_tab[j], 16)
            with sp.Fori(1, TILES) as i:
                for j in range(4):
                    sp.wait_ge(tab_turned, i * 4 + (j - 3))
                    sp.dma_start(tab[:, j, :], down_rows[:, ds(i * 4 + j, 1), :].rearrange("p c d -> p (c d)")
                                 ).then_inc(in_tab[j], 16)
            for j in range(4):
                sp.wait_ge(tab_turned, CHUNKS - 3 + j)
                sp.dma_start(tab[:, j, :], up_rows[:, j, :]).then_inc(in_tab[j], 16)
            for half in range(2):
                with sp.Fori(1 - half, TILES) as i:
                    for j in range(4):
                        sp.wait_ge(chunk_used, i * 4 + (CHUNKS * half + j - 3))
                        sp.dma_start(tab[:, j, :], up_rows[:, ds(i * 4 + j, 1), :].rearrange("p c d -> p (c d)")
                                     ).then_inc(in_tab[j], 16)
            out_rows = out.rearrange("b n d -> (b n) d")
            for t in range(TILES):
                sp.wait_ge(result_ready, t + 1)
                sp.dma_start(out_rows[t * P:(t + 1) * P, :], result[:, t % 2, :]).then_inc(stored[t % 2], 16)
            for u in range(2):
                sp.wait_ge(stored[u], 16 * TILES // 2)

        @block.gpsimd
        def _(pool):
            pool.memset(keysB, 0.0).then_inc(pool_ready, 1)
            pool.memset(minus_half[:, :], -0.5).then_inc(pool_ready, 1)
            pool.iota(iota8[:, :], [[1, TOPK]], base=0, channel_multiplier=0,
                      allow_small_or_imprecise_dtypes=True).then_inc(pool_ready, 1)
            pool.iota(grid[:, :, :], [[1, KEYS], [0, STEP]], base=0, channel_multiplier=0,
                      allow_small_or_imprecise_dtypes=True).then_inc(pool_ready, 1)
            for l in range(2):
                for c in range(CHANNELS):
                    pool.wait_ge(in_x[l][c], 32)
                    pool.tensor_copy(x_feats[:, c, l, :, :].rearrange("p w (i j) -> p w i j", j=PATCH),
                                     x_rows[:, c, l, :].rearrange("p (i w j) -> p w i j", w=GRID, j=PATCH)
                                     ).then_inc(x_sorted, 1)
            pool.wait_ge(h0T_ready, 4)
            for u in range(2):
                pool.tensor_copy(h0s[:, u, :, :], h0T[:, :, u * P:(u + 1) * P]).then_inc(h0s_ready, 1)
            pool.wait_ge(pool_ready, 4)
            with pool.Fori(0, TILES // 2) as i:
                for u in range(2):
                    pool.wait_ge(scored, i * 2 + (u + 1))
                    following = (i * 2 + (u + 2)) % TILES
                    pool.tensor_copy(h0s[:, u, :, :], h0T[:, :, ds(following * P, P)]).then_inc(h0s_ready, 1)
                for u in range(2):
                    pool.wait_ge(var_ready, i * 2 + (u + 1))
                    pool.tensor_tensor(stat(u, RSTD), stat(u, VAR_EPS), minus_half[:, :],
                                       ALU.pow).then_inc(rstd_ready, 1)
                for u in range(2):
                    pool.wait_ge(h1s_ready, i * 2 + (u + 1))
                    pool.tensor_copy(h1[:, ds(i * 2 + u, 1), :].rearrange("p t d -> p (t d)"), h1s[:, u, :]
                                     ).then_inc(h1_ready, 1)
            for t in range(TILES):
                pool.wait_ge(var2_ready, t + 1)
                pool.tensor_tensor(stat(t % 2, RSTD), stat(t % 2, VAR_EPS), minus_half[:, :],
                                   ALU.pow).then_inc(rstd2_ready, 1)

        @block.tensor
        def _(pe):
            def turn_group(g):
                _, blocks, _, arrived, value = groups[g]
                pe.wait_ge(arrived, value)
                if g >= 4 and g % 2 == 0:
                    pe.wait_ge(turned_by_act, (g - 4) // 2 + 1)
                elif g >= 4:
                    pe.wait_ge(turned_by_dve, (g - 4) // 2 + 1)
                for n, b in enumerate(blocks):
                    last = pe.transpose(turn[g % 4][:, n * P:(n + 1) * P], b, ident[:, :])
                last.then_inc(turned, 1)

            def embed(l, groups_before):
                pe.wait_ge(turned_by_act, act_groups(groups_before))
                pe.wait_ge(turned_by_dve, groups_before - act_groups(groups_before))
                for o in range(DK):
                    for k in range(FK):
                        last = pe.matmul(bank[2 * l + o][:, :], tokwT[:, k, o * P:(o + 1) * P], xT[:, l, k, :],
                                         start=(k == 0), stop=(k == FK - 1))
                    last.then_inc(embedded, 1)

            pe.wait_ge(in_const, 64)
            pe.wait_ge(pos_biased, 1)
            for k in range(DK):
                last = pe.transpose(bank[3][:, k * PATCHES:(k + 1) * PATCHES],
                                    pos_nat[0:PATCHES, k * P:(k + 1) * P], ident[0:PATCHES, 0:PATCHES])
            last.then_inc(pos_turned, 1)
            for g in range(x1_starts):
                turn_group(g)
            embed(0, x1_starts)
            for g in range(x1_starts, weights_start):
                turn_group(g)
            pe.wait_ge(posT_ready, 1)
            embed(1, weights_start)
            for g in range(weights_start, n_groups):
                turn_group(g)
            pe.wait_ge(turned_by_act, act_groups(n_groups))
            pe.wait_ge(turned_by_dve, n_groups - act_groups(n_groups))
            for s in range(2):
                last = pe.transpose(turn[0][:, s * P:(s + 1) * P], keys_nat[:, s, :], ident[:, :])
            last.then_inc(keys_turned, 1)

            pe.wait_ge(keysB_ready, 4)
            pe.wait_ge(h0T_ready, 4)
            with pe.Fori(0, TILES // 2) as i:
                for u in range(2):
                    pe.wait_ge(h0s_ready, i * 2 + (u + 1))
                    for o in range(DK):
                        for k in range(DK):
                            pe.matmul(bank[u][:, o * P:(o + 1) * P], attnwT[:, k, o * P:(o + 1) * P],
                                      h0s[:, u, k, :], start=(k == 0), stop=(k == DK - 1))
                    for k in range(DK):
                        last = pe.matmul(bank[u][:, D:2 * D], h0s[:, u, k, :], attnwT[:, k, D:2 * D],
                                         start=(k == 0), stop=(k == DK - 1))
                    last.then_inc(kv_done, 1)
                    for k in range(DK):
                        last = pe.transpose(region[u][:, k * P:(k + 1) * P], h0s[:, u, k, :], ident[:, :])
                    last.then_inc(kv_done, 1)
                for u in range(2):
                    pe.wait_ge(kv_ready, i * 2 + (u + 1))
                    pe.wait_ge(h0x2_ready, i * 2 + (u + 1))
                    for k in range(DK):
                        last = pe.matmul(region[u][:, 256:384], h0s[:, u, k, :], kv[:, u, k * P:(k + 1) * P],
                                         start=(k == 0), stop=(k == DK - 1))
                    last.then_inc(scored, 1)
                for u in range(2):
                    pe.wait_ge(probs_ready, i * 2 + (u + 1))
                    pe.transpose(region[u][:, 384:512], probs[:, u, :], ident[:, :]).then_inc(probs_turned, 1)
                for u in range(2):
                    pe.wait_ge(probsT_ready, i * 2 + (u + 1))
                    pe.matmul(region[u][:, 512:768], probsT[:, u, :], kv[:, u, D:2 * D],
                              start=True, stop=True).then_inc(attended, 1)
                for u in range(2):
                    pe.wait_ge(h1s_ready, i * 2 + (u + 1))
                    for k in range(DK):
                        last = pe.transpose(region[u][:, 768 + k * P:768 + (k + 1) * P],
                                            h1s[:, u, k * P:(k + 1) * P], ident[:, :])
                    last.then_inc(h1_turned, 1)

            pe.wait_ge(h1T_ready, TILES)
            with pe.Fori(0, TILES) as i:
                def turn_chunk(j):
                    pe.wait_ge(in_tab[j], i * 16 + 16)
                    for k in range(DK):
                        last = pe.transpose(bank[j % 2][:, k * P:(k + 1) * P],
                                            tab[:, j, k * P:(k + 1) * P], ident[:, :])
                    last.then_inc(tab_turned, 1)

                def dots(j):
                    pe.wait_ge(dT_ready, i * 4 + (j + 1))
                    for half in range(2):
                        if j > 0:
                            pe.wait_ge(S_ready, i * 8 + (2 * j + half - 1))
                        for k in range(DK):
                            last = pe.matmul(bank[2 + half][:, :], dT[:, j % 2, k, :],
                                             h1T[:, k, half * HALF:(half + 1) * HALF],
                                             start=(k == 0), stop=(k == DK - 1))
                        last.then_inc(dots_done, 1)

                turn_chunk(0)
                for s in range(2):
                    for k in range(DK):
                        last = pe.matmul(region[1][:, s * P:(s + 1) * P], querywT[:, k, s * P:(s + 1) * P],
                                         h1T[:, k, ds(i * P, P)], start=(k == 0), stop=(k == DK - 1))
                last.then_inc(query_done, 1)
                turn_chunk(1)
                dots(0)
                pe.wait_ge(qs_ready, i + 1)
                for s in range(2):
                    last = pe.matmul(region[0][:, s * 512:(s + 1) * 512], qs[:, s, :], keysB[:, s, :],
                                     start=True, stop=True)
                last.then_inc(sim_done, 1)
                turn_chunk(2)
                dots(1)
                turn_chunk(3)
                dots(2)
                dots(3)
                pe.wait_ge(sims_read, i + 1)

            def build_C(n, parity):
                pe.wait_ge(onehots_ready, n + 1)
                for g in range(2):
                    pe.wait_ge(region_free, n * 2 + (g + 1))
                    for s in range(STEP):
                        for part in range(2):
                            last = pe.matmul(region[g][:, s * 64:(s + 1) * 64],
                                             onehot_y[64 * g:64 * g + 64, parity, :, s],
                                             weighted_x[64 * g:64 * g + 64, parity, 2 * part:2 * part + 2, :, s],
                                             start=(part == 0), stop=(part == 1))
                    last.then_inc(region_done, 1)

            pe.wait_ge(S_ready, 2 * CHUNKS)
            with pe.Fori(0, 2) as half:
                for q in range(MK):
                    for b, w in ((0, gatewT), (1, upwT)):
                        pe.wait_ge(hidden_free, half * MK + (q + 1))
                        for k in range(DK):
                            last = pe.matmul(bank[b][:, :], w[:, k, q * P:(q + 1) * P],
                                             h1T[:, k, ds(half * HALF, HALF)], start=(k == 0), stop=(k == DK - 1))
                        last.then_inc(gates_done, 1)
                    build_C(half * MK + q, q % 2)

            def add_mlp(half, blocks):
                for fk in blocks:
                    for o in range(DK):
                        last = pe.matmul(sums[half][o], downwT[:, fk, o * P:(o + 1) * P],
                                         mT[:, fk, half * HALF:(half + 1) * HALF],
                                         start=(fk == 0), stop=(fk == MK - 1), skip_group_check=True)
                return last

            def add_chunks(half, i, base):
                for j in range(4):
                    pe.wait_ge(in_tab[j], base)
                    for o in range(DK):
                        last = pe.matmul(sums[half][o], tab[:, j, o * P:(o + 1) * P],
                                         S[:, ds(i * 4 + j, 1), half * HALF:(half + 1) * HALF]
                                         .rearrange("p c t -> p (c t)"),
                                         start=False, stop=False, skip_group_check=True)
                    last.then_inc(chunk_used, 1)

            def turn_output(half):
                pe.wait_ge(outT_ready, DK * (half + 1))
                if half:
                    pe.wait_ge(result_ready, TILES // 2)
                for t in range(TILES // 2 * half, TILES // 2 * (half + 1)):
                    a = t % (TILES // 2) * P
                    for o in range(DK):
                        last = pe.transpose(out_slot(t)[:, o * P:(o + 1) * P], outT[:, o, a:a + P], ident[:, :])
                    last.then_inc(out_turned, 1)

            pe.wait_ge(hidden_free, 2 * MK + 1)
            add_mlp(0, (0, 1))
            pe.wait_ge(region_free, HALF_TILES + 2)
            with pe.Fori(0, TILES // 2) as i:
                for q in range(2):
                    add_chunks(0, i * 2 + q, i * 32 + 16 * (TILES + q + 1))
                    build_C(i * 2 + (HALF_TILES // 2 + q), q)
            add_mlp(0, (2, 3)).then_inc(summed, 1)
            add_mlp(1, (0, 1))
            pe.wait_ge(region_free, 2 * HALF_TILES + 2)
            turn_output(0)
            with pe.Fori(0, TILES) as i:
                add_chunks(1, i, i * 16 + 16 * (2 * TILES + 1))
            add_mlp(1, (2, 3)).then_inc(summed, 1)
            turn_output(1)

        @block.scalar
        def _(act):
            for g in range(0, n_groups, 2):
                act.wait_ge(turned, g + 1)
                if names[g] == "queryw":
                    act.wait_ge(pool_ready, 1)
                act.copy(groups[g][2], turn[g % 4]).then_inc(turned_by_act, 1)
            act.wait_ge(keys_turned, 1)
            act.wait_ge(pool_ready, 1)
            for h in range(HEADS):
                act.copy(keysB[RET * h:RET * (h + 1), :, h * KEYS:(h + 1) * KEYS],
                         turn[0][RET * h:RET * (h + 1), 0:256].rearrange("p (s k) -> p s k", s=2)
                         ).then_inc(keysB_ready, 1)

            with act.Fori(0, TILES // 2) as i:
                for u in range(2):
                    act.wait_ge(kv_done, i * 4 + (2 * u + 1))
                    act.copy(kv[:, u, :], bank[u][:, :]).then_inc(kv_ready, 1)
                    act.wait_ge(kv_done, i * 4 + (2 * u + 2))
                    act.mul(h0x2[:, u, :], region[u][:, 0:256], 2.0).then_inc(h0x2_ready, 1)
                for u in range(2):
                    act.wait_ge(max_ready, i * 2 + (u + 1))
                    act.activation(probs[:, u, :], masked[:, u, :], ACT.Exp, bias=stat(u, NEG_MAX),
                                   accum_out=stat(u, SUM)).then_inc(probs_ready, 1)
                for u in range(2):
                    act.wait_ge(probs_turned, i * 2 + (u + 1))
                    act.copy(probsT[:, u, :], region[u][:, 384:512]).then_inc(probsT_ready, 1)
                for u in range(2):
                    act.wait_ge(h1_turned, i * 2 + (u + 1))
                    act.copy(h1T[:, :, ds((i * 2 + u) * P, P)],
                             region[u][:, 768:1024].rearrange("p (k t) -> p k t", k=DK)).then_inc(h1T_ready, 1)

            act.wait_ge(h0s_ready, TILES + 2)
            with act.Fori(0, TILES) as i:
                def chunk_out(j):
                    act.wait_ge(tab_turned, i * 4 + (j + 1))
                    if j >= 2:
                        act.wait_ge(dots_done, i * 8 + (2 * j - 2))
                    act.copy(dT[:, j % 2, :, :], bank[j % 2][:, 0:256].rearrange("p (k t) -> p k t", k=DK)
                             ).then_inc(dT_ready, 1)

                def silu(j):
                    for half in range(2):
                        act.wait_ge(dots_done, i * 8 + (2 * j + half + 1))
                        act.activation(S[:, ds(i * 4 + j, 1), half * HALF:(half + 1) * HALF]
                                       .rearrange("p c t -> p (c t)"), bank[2 + half][:, :], ACT.Silu
                                       ).then_inc(S_ready, 1)

                chunk_out(0)
                act.wait_ge(query_done, i + 1)
                act.copy(qs, region[1][:, 0:256].rearrange("p (s t) -> p s t", s=2)).then_inc(qs_ready, 1)
                chunk_out(1)
                silu(0)
                chunk_out(2)
                silu(1)
                chunk_out(3)
                silu(2)
                silu(3)
            act.wait_ge(diffs_ready, TILES)
            act.activation(exps, diffs, ACT.Exp).then_inc(exps_ready, 1)

            with act.Fori(0, 2) as half:
                for q in range(MK):
                    act.wait_ge(gates_done, half * (2 * MK) + (2 * q + 1))
                    act.wait_ge(hidden_free, half * MK + (q + 1))
                    act.activation(gate_out, bank[0][:, :], ACT.Silu).then_inc(gate_ready, 1)

            for half in range(2):
                act.wait_ge(summed, half + 1)
                if half:
                    act.wait_ge(out_turned, TILES // 2)
                for o in range(DK):
                    act.mul(outT[:, o, :], sums[half][o], 1.0 / WSCALE).then_inc(outT_ready, 1)

        @block.vector
        def _(dve):
            steps = [0]

            def step(ins):
                steps[0] += 1
                ins.then_inc(dve_step, 1)
                dve.wait_ge(dve_step, steps[0])

            def hold():
                dve.memset(held[:, :], 0.0)

            def embed_out(l):
                for o in range(DK):
                    dve.wait_ge(embedded, 2 * l + o + 1)
                    dve.tensor_tensor(
                        h0T[:, o, :].rearrange("p (b q l w) -> p l w q b", q=2, l=2, w=GRID)[:, l],
                        bank[2 * l + o][:, :].rearrange("p (w q b) -> p w q b", w=GRID, q=2),
                        posT[:, o, :].rearrange("p (q l w) -> p l w q", q=2, l=2)[:, l].unsqueeze(3)
                        .broadcast_to([P, GRID, 2, IMAGES]), ALU.add).then_inc(h0T_ready, 1)

            def take_out(first, end):
                for g in range(first + (first + 1) % 2, end, 2):
                    dve.wait_ge(turned, g + 1)
                    dve.tensor_copy(groups[g][2], turn[g % 4]).then_inc(turned_by_dve, 1)

            dve.wait_ge(in_const, 64)
            dve.tensor_tensor(pos_nat[0:PATCHES, :], pos_nat[0:PATCHES, :], bias_rows[0:PATCHES, :], ALU.add
                              ).then_inc(pos_biased, 1)
            dve.wait_ge(pos_turned, 1)
            dve.tensor_copy(posT, bank[3][:, 0:DK * PATCHES].rearrange("p (k n) -> p k n", k=DK)
                            ).then_inc(posT_ready, 1)
            dve.wait_ge(posT_ready, 1)
            take_out(0, x1_starts)
            embed_out(0)
            take_out(x1_starts, weights_start)
            embed_out(1)
            take_out(weights_start, n_groups)

            dve.sem_inc(hidden_free, 1)
            dve.sem_inc(region_free, 2)

            dve.wait_ge(in_rest, in_rest_all)
            loop_base = steps[0]
            per_turn = 2 * 5
            with dve.Fori(0, TILES // 2) as i:
                n = [0]

                def chain(ins):
                    n[0] += 1
                    ins.then_inc(dve_step, 1)
                    dve.wait_ge(dve_step, i * per_turn + (loop_base + n[0]))

                for u in range(2):
                    dve.wait_ge(scored, i * 2 + (u + 1))
                    chain(dve.tensor_tensor(masked[:, u, :], region[u][:, 256:384], mask, ALU.add))
                    dve.tensor_reduce(stat(u, NEG_MAX), masked[:, u, :], AX_X, ALU.max, negate=True
                                      ).then_inc(max_ready, 1)
                for u in range(2):
                    dve.wait_ge(probs_ready, i * 2 + (u + 1))
                    dve.wait_ge(h0x2_ready, i * 2 + (u + 1))
                    chain(dve.reciprocal(stat(u, RECIP), stat(u, SUM)))
                    dve.wait_ge(attended, i * 2 + (u + 1))
                    chain(dve.scalar_tensor_tensor(y1[:, u, :], region[u][:, 512:768], stat(u, RECIP),
                                                   h0x2[:, u, :], ALU.mult, ALU.add))
                    chain(dve.bn_stats(stat(u, STATS, 6), y1[:, u, :]))
                    hold()
                    chain(dve.bn_aggr(stat(u, MEAN, 2), stat(u, STATS, 6)))
                    dve.tensor_scalar(stat(u, VAR_EPS), stat(u, VAR), EPS, None, ALU.add).then_inc(var_ready, 1)
                for u in range(2):
                    dve.wait_ge(rstd_ready, i * 2 + (u + 1))
                    dve.tensor_scalar(h1s[:, u, :], y1[:, u, :], stat(u, MEAN), stat(u, RSTD),
                                      ALU.subtract, ALU.mult).then_inc(h1s_ready, 1)
                assert n[0] == per_turn
            steps[0] += per_turn * (TILES // 2)

            loop_base2 = steps[0]
            per_tile = 10
            dve.wait_ge(pool_ready, 4)
            with dve.Fori(0, TILES) as i:
                n = [0]

                def chain(ins):
                    n[0] += 1
                    ins.then_inc(dve_step, 1)
                    dve.wait_ge(dve_step, i * per_tile + (loop_base2 + n[0]))

                def sims(s, h):
                    return region[0][:, s * 512 + h * KEYS:s * 512 + (h + 1) * KEYS]

                pairs = [(s, h) for s in range(2) for h in range(HEADS)]
                dve.wait_ge(sim_done, i + 1)
                hold()
                for s, h in pairs:
                    last = dve.max(top_val[:, s, h, :], sims(s, h))
                chain(last)
                hold()
                for s, h in pairs:
                    last = dve.max_index(top_idx[:, s, h, :], top_val[:, s, h, :], sims(s, h))
                last.then_inc(sims_read, 1)
                chain(dve.tensor_tensor(
                    pair_sum.rearrange("p (h i j) -> p h i j", h=HEADS, i=TOPK),
                    top_val[:, 0].unsqueeze(3).broadcast_to([P, HEADS, TOPK, TOPK]),
                    top_val[:, 1].unsqueeze(2).broadcast_to([P, HEADS, TOPK, TOPK]), ALU.add))
                hold()
                for h in range(HEADS):
                    last = dve.max(pair_val[:, h, :], pair_sum[:, h * 64:(h + 1) * 64])
                chain(last)
                hold()
                for h in range(HEADS):
                    last = dve.max_index(pair_pos[:, h * TOPK:(h + 1) * TOPK], pair_val[:, h, :],
                                         pair_sum[:, h * 64:(h + 1) * 64])
                chain(last)
                dve.tensor_tensor(diffs[:, ds(i, 1), :].rearrange("p t (h k) -> p (t h) k", h=HEADS), pair_val[:, :, :],
                                  pair_val[:, :, 0:1].broadcast_to([P, HEADS, TOPK]), ALU.subtract
                                  ).then_inc(diffs_ready, 1)
                dve.tensor_scalar(pair_ij[:, 0, :], pair_pos[:, :], 3, None, ALU.logical_shift_right)
                chain(dve.tensor_scalar(pair_ij[:, 1, :], pair_pos[:, :], TOPK - 1, None, ALU.bitwise_and))
                chain(dve.tensor_tensor(
                    match, pair_ij[:, :, :].rearrange("p s a -> p (s a)").unsqueeze(2)
                    .broadcast_to([P, 2 * PICKS, TOPK]),
                    iota8[:, :].unsqueeze(1).broadcast_to([P, 2 * PICKS, TOPK]), ALU.is_equal))
                dve.wait_ge(sims_read, i + 1)
                chain(dve.tensor_tensor(
                    picked.rearrange("p (g k) i -> p g k i", k=TOPK),
                    match.rearrange("p (g k) i -> p g k i", k=TOPK),
                    top_idx[:, :, :, :].rearrange("p s h i -> p (s h) i").unsqueeze(2)
                    .broadcast_to([P, 2 * HEADS, TOPK, TOPK]), ALU.mult))
                chain(dve.tensor_reduce(row_xy[:, :, :].rearrange("p s a -> p (s a)"), picked, AX_X, ALU.add))
                chain(dve.tensor_scalar(edge[:, :], row_xy[:, 0, :], float(CHUNKS), float(KEYS - 1),
                                        ALU.is_ge, ALU.mult))
                dve.tensor_scalar(pack[:, ds(i, 1), 0, :].rearrange("p t a -> p (t a)"), row_xy[:, 0, :],
                                  float(CHUNKS - 1), None, ALU.min)
                chain(dve.tensor_tensor(pack[:, ds(i, 1), 1, :].rearrange("p t a -> p (t a)"), row_xy[:, 1, :],
                                        edge[:, :], ALU.max))
                assert n[0] == per_tile, n[0]
            steps[0] += per_tile * TILES

            heads = "p t (h k) -> p (t h) k"
            sums8 = top_val[:, :, :, :].rearrange("p s h k -> p (s h k)")[:, 0:32]
            recips = top_val[:, :, :, :].rearrange("p s h k -> p (s h k)")[:, 32:64]
            dve.wait_ge(exps_ready, 1)
            step(dve.tensor_reduce(sums8, exps.rearrange(heads, h=HEADS), AX_X, ALU.add))
            step(dve.reciprocal(recips, sums8))
            step(dve.scalar_tensor_tensor(diffs.rearrange(heads, h=HEADS), exps.rearrange(heads, h=HEADS), WSCALE,
                                          recips.unsqueeze(2).broadcast_to([P, TILES * HEADS, TOPK]),
                                          ALU.mult, ALU.mult))
            step(dve.tensor_copy(pack[:, :, 2, :], diffs))
            step(dve.tensor_tensor(pack[:, :, 3, :], diffs, pack[:, :, 2, :], ALU.subtract))
            step(dve.transpose(selT[:, :, :, :].rearrange("p t q s -> p (t q s)"),
                               pack.rearrange("p t q a -> p (t q a)")))
            for slot in range(2):
                last = dve.tensor_scalar(selW[:, :, :, slot, :], selT[:, :, 2:4, :], slot_mask[:, slot:slot + 1],
                                         None, ALU.mult)
            step(last)

            def onehots(tile, hf, x_done):
                cols = slice(STEP * hf, STEP * (hf + 1))
                dve.tensor_tensor(onehot_x[:, hf, :, :], grid[:, 0:32, :],
                                  selT[:, tile, 0, cols].broadcast_to([P, 32, STEP]), ALU.is_equal
                                  ).then_inc(dve_step, 1)
                dve.tensor_tensor(onehot_y[:, hf, :, :], grid[:, :, :],
                                  selT[:, tile, 1, cols].broadcast_to([P, KEYS, STEP]), ALU.is_equal)
                dve.wait_ge(dve_step, x_done)
                dve.tensor_tensor(weighted_x[:, hf, :, :, :],
                                  onehot_x[:, hf:hf + 1, :, :].broadcast_to([P, 4, 32, STEP]),
                                  selW[:, tile, :, :, cols].rearrange("p t a b s -> p (t a b) s").unsqueeze(2)
                                  .broadcast_to([P, 4, 32, STEP]), ALU.mult).then_inc(onehots_ready, 1)

            S_tiles = S[:, :, :].rearrange("p x (n b t) -> p x n b t", n=TILES, b=4)

            def multiply(tile, hf, n):
                for g in range(2):
                    dve.wait_ge(region_done, n * 2 + (g + 1))
                    block_S = S_tiles[:, :, tile, 2 * g:2 * g + 2, STEP * hf:STEP * (hf + 1)].rearrange(
                        "p x n b t -> p x (n b) t")
                    dve.tensor_tensor(block_S, region[g][:, :].rearrange("p (s b x) -> p x b s", s=STEP, b=2),
                                      block_S, ALU.mult).then_inc(region_free, 1)

            def one(tile):
                return slice(tile, tile + 1) if isinstance(tile, int) else ds(tile, 1)

            for hf in range(2):
                steps[0] += 1
                onehots(one(0), hf, steps[0])
            dve.wait_ge(S_ready, 2 * CHUNKS)
            dve.wait_ge(h1_ready, TILES)
            dve.wait_ge(h0s_ready, TILES + 2)
            base = steps[0]
            with dve.Fori(0, 2) as half:
                for q in range(MK):
                    n = half * MK + q
                    dve.wait_ge(gate_ready, n + 1)
                    dve.wait_ge(gates_done, n * 2 + 2)
                    dve.scalar_tensor_tensor(mT[:, q, ds(half * HALF, HALF)], gate_out, WSCALE, bank[1][:, :],
                                             ALU.mult, ALU.mult).then_inc(hidden_free, 1)
                    tile = half * 2 + q // 2
                    multiply(one(tile), q % 2, n)
                    onehots(one(tile + 1), q % 2, half * MK + (base + q + 1))
            steps[0] += 2 * MK
            base = steps[0]
            with dve.Fori(0, TILES // 2 - 1) as i:
                for q in range(2):
                    tile = i + TILES // 2
                    multiply(one(tile), q, tile * 2 + q)
                    onehots(one(tile + 1), q, i * 2 + (base + q + 1))
            steps[0] += 2 * (TILES // 2 - 1)
            for q in range(2):
                multiply(one(TILES - 1), q, 2 * (TILES - 1) + q)

            for t in range(TILES):
                u = t % 2
                dve.wait_ge(out_turned, t + 1)
                step(dve.tensor_tensor(y2[:, u, :], out_slot(t), h1[:, t, :], ALU.add))
                step(dve.bn_stats(stat(u, STATS, 6), y2[:, u, :]))
                step(dve.bn_aggr(stat(u, MEAN, 2), stat(u, STATS, 6)))
                dve.tensor_scalar(stat(u, VAR_EPS), stat(u, VAR), EPS, None, ALU.add).then_inc(var2_ready, 1)
                dve.wait_ge(rstd2_ready, t + 1)
                if t >= 2:
                    dve.wait_ge(stored[u], 16 * (t // 2))
                dve.tensor_scalar(result[:, u, :], y2[:, u, :], stat(u, MEAN), stat(u, RSTD),
                                  ALU.subtract, ALU.mult).then_inc(result_ready, 1)


_ARGS = ["x", "L0_tok_W", "L0_tok_b", "L0_tok_pos_emb", "L0_attn_W", "L0_ffn_w_queries", "L0_ffn_keys",
         "L0_ffn_down_embed", "L0_ffn_up_embed", "L0_ffn_w_gate", "L0_ffn_w_up", "L0_ffn_w_down"]


def constant_tables():
    import numpy as np

    row = np.arange(P)
    image, patch = row // PATCHES, row % PATCHES
    seen = (image[:, None] == image[None, :]) & (patch[None, :] <= patch[:, None])
    quadrant = row // 32
    return np.concatenate([np.eye(P), np.where(seen, 0.0, -3e38),
                           quadrant[:, None] % 2 == np.arange(2)[None, :]], axis=1).astype(np.float32)


def kernel(**inputs):
    import numpy as np
    import concourse.bacc as bacc
    from concourse.bass_utils import run_bass_kernel_spmd

    nc = bacc.Bacc("TRN2", target_bir_lowering=False, num_devices=1)
    arrays, args = {}, []
    named = [(name, np.ascontiguousarray(inputs[name])) for name in _ARGS] + [("constants", constant_tables())]
    for name, a in named:
        arrays[f"in_{name}"] = a
        args.append(nc.dram_tensor(f"in_{name}", a.shape, mybir.dt.from_np(a.dtype), kind="ExternalInput").ap())
    out = nc.dram_tensor("out_h", (IMAGES, PATCHES, D), F32, kind="ExternalOutput").ap()
    vit_block_kernel(nc, *args, out)
    run = run_bass_kernel_spmd(nc, [arrays], core_ids=[0])
    return run.results[0]["out_h"]
```

```python
from contextlib import ExitStack

import concourse.bass as bass
from concourse import mybir

P = 128
IMAGES, CHANNELS, SIDE, PATCH = 64, 3, 64, 16
GRID = SIDE // PATCH
PATCHES = GRID * GRID
D = 256
DK = D // P
TOKENS = IMAGES * PATCHES
TILES = TOKENS // P
TILE_IMAGES = P // PATCHES
FEATURES = CHANNELS * PATCH * PATCH
FK = FEATURES // P
HALF = TOKENS // 2
HEADS, TOPK, KEYS = 4, 8, 128
PICKS = HEADS * TOPK
RET = 32
EXPERTS = 4096
CHUNKS = EXPERTS // P
INTER = 512
MK = INTER // P
EPS = 1e-5
WSCALE = float(2 ** 14)
CHUNKS_PER_TILE = CHUNKS // TILES
STEP = 16
HALF_TILES = 2 * TILES

ALU = mybir.AluOpType
ACT = mybir.ActivationFunctionType
AX_X = mybir.AxisListType.X
F32 = mybir.dt.float32
F16 = mybir.dt.float16
F32R = mybir.dt.float32r
U32 = mybir.dt.uint32
ds = bass.ds


def vit_block_kernel(nc, x, tok_w, tok_b, pos_emb, attn_w, w_queries, keys, down_embed, up_embed,
                     w_gate, w_up, w_down, constants, out):
    with ExitStack() as ctx:
        def sb(name, shape, dt):
            return ctx.enter_context(nc.sbuf_tensor(name, shape, dt))

        def sem(name):
            return ctx.enter_context(nc.semaphore(name))

        def shared(*sets):
            handles = []
            for tensors in sets[:-1]:
                with ExitStack() as phase:
                    handles.append([phase.enter_context(nc.sbuf_tensor(*t)) for t in tensors])
            handles.append([sb(*t) for t in sets[-1]])
            return handles

        S = sb("S", [P, CHUNKS, TOKENS], F32)
        S_flat = S[:, :, :].rearrange("p c t -> p (c t)")
        at = [0]

        def early(cols):
            at[0] += cols
            return S_flat[:, at[0] - cols:at[0]]

        x_rows_flat = early(CHANNELS * 2 * PATCH * SIDE)
        x_rows = x_rows_flat.rearrange("p (c l m) -> p c l m", c=CHANNELS, l=2)
        x_feats = early(CHANNELS * 2 * PATCH * SIDE).rearrange("p (c l w f) -> p c l w f", c=CHANNELS, l=2, w=GRID)
        xT = early(2 * FK * HALF).rearrange("p (l k t) -> p l k t", l=2, k=FK)
        tokw_nat = early(DK * FEATURES).rearrange("p (o f) -> p o f", o=DK)
        attnw_nat = early(2 * DK * D).rearrange("p (o f) -> p o f", f=D)
        queryw_nat = early(DK * D).rearrange("p (o f) -> p o f", f=D)
        gatew_nat = early(MK * D).rearrange("p (o f) -> p o f", f=D)
        upw_nat = early(MK * D).rearrange("p (o f) -> p o f", f=D)
        downw_nat = early(DK * INTER).rearrange("p (o f) -> p o f", f=INTER)
        keys_nat = early(2 * P).rearrange("p (s f) -> p s f", f=P)
        pos_nat = early(D)
        tokwT = early(FK * D).rearrange("p (k o) -> p k o", o=D)
        attnwT = early(DK * 2 * D).rearrange("p (k o) -> p k o", o=2 * D)
        h0T = early(DK * TOKENS).rearrange("p (k t) -> p k t", t=TOKENS)
        posT = early(DK * PATCHES).rearrange("p (k n) -> p k n", n=PATCHES)
        bias_rows = early(D)
        mask = early(P)
        at_x = [0]

        def pair(cols):
            at_x[0] += 2 * cols
            return x_rows_flat[:, at_x[0] - 2 * cols:at_x[0]].rearrange("p (u f) -> p u f", u=2)

        h0s = pair(D).rearrange("p u (k t) -> p u k t", k=DK)
        kv = pair(2 * D)
        h0x2 = pair(D)
        masked = pair(P)
        probs = pair(P)
        probsT = pair(P)
        y1 = pair(D)
        h1s = pair(D)

        downwT = sb("downwT", [P, MK, D], F32)
        h1T = sb("h1T", [P, DK, TOKENS], F32)
        h1 = sb("h1", [P, TILES, D], F32)
        grid = sb("grid", [P, KEYS, STEP], F16)
        ident = sb("ident", [P, P], F32)
        slot_mask = sb("slot_mask", [P, 2], F32)
        iota8 = sb("iota8", [P, TOPK], F32)
        minus_half = sb("minus_half", [P, 1], F32)
        tab = sb("tab", [P, 4, D], F32)
        dT = sb("dT", [P, 2, DK, P], F32)
        selT = sb("selT", [P, TILES, 4, 32], F16)
        selW = sb("selW", [P, TILES, 2, 2, 32], F16)
        held = sb("held", [P, 2], F32)
        small = sb("small", [P, 64], F32)
        edge = sb("edge", [P, PICKS], F32)

        (h1T_hi, h1T_lo), (mT,) = shared(
            [("h1T_hi", [P, DK, TOKENS], F32R), ("h1T_lo", [P, DK, TOKENS], F32R)],
            [("mT", [P, MK, TOKENS], F32)])
        (up_hi, up_lo), (gatewT, upwT) = shared(
            [("up_hi", [P, 4, D], F32R), ("up_lo", [P, 4, D], F32R)],
            [("gatewT", [P, DK, INTER], F32), ("upwT", [P, DK, INTER], F32)])
        (keysB_t, querywT_t, qs_t, match_t, pair_sum_t, diffs_t, dT_hi, dT_lo), (G_hi, G_lo), \
            (onehot_y, weighted_x) = shared(
                [("keysB", [P, 2, HEADS * KEYS], F32), ("querywT", [P, DK, D], F32), ("qs", [P, 2, P], F32),
                 ("match", [P, 2 * PICKS, TOPK], F32), ("pair_sum", [P, HEADS * TOPK * TOPK], F32),
                 ("diffs", [P, TILES, PICKS], F32), ("dT_hi", [P, 2, DK, P], F32R), ("dT_lo", [P, 2, DK, P], F32R)],
                [("G_hi", [P, 4, HALF], F32R), ("G_lo", [P, 4, HALF], F32R)],
                [("onehot_y", [P, 2, KEYS, STEP], F16), ("weighted_x", [P, 2, 4, 32, STEP], F16)])
        keysB, querywT, qs = keysB_t[:, :, :], querywT_t[:, :, :], qs_t[:, :, :]
        querywT_flat = querywT.rearrange("p k o -> p (k o)")
        match, pair_sum, diffs = match_t[:, :, :], pair_sum_t[:, :], diffs_t[:, :, :]
        exps = match.rearrange("p a i -> p (a i)")[:, 0:TILES * PICKS].rearrange("p (t a) -> p t a", a=PICKS)
        onehot_x = sb("onehot_x", [P, 2, 32, STEP], F16)
        pack = onehot_x[:, :, :, :].rearrange("p u x s -> p (u x s)").rearrange(
            "p (t q a) -> p t q a", q=4, a=PICKS)

        top_val = sb("top_val", [P, 2, HEADS, TOPK], F32)
        top_idx = sb("top_idx", [P, 2, HEADS, TOPK], U32)
        pair_val = sb("pair_val", [P, HEADS, TOPK], F32)
        pair_pos = sb("pair_pos", [P, PICKS], U32)
        pair_ij = sb("pair_ij", [P, 2, PICKS], U32)
        row_xy = sb("row_xy", [P, 2, PICKS], F32)

        late = h1T[:, :, :].rearrange("p k t -> p (k t)")
        outT = late[:, 0:1024].rearrange("p (k t) -> p k t", k=DK)
        result = late[:, 1024:2048].rearrange("p (r f) -> p r f", r=4)

        bank = [ctx.enter_context(nc.psum_tensor(f"bank{i}", [P, 512], F32)) for i in range(4)]
        region = [ctx.enter_context(nc.psum_tensor(f"region{i}", [P, 1024], F32)) for i in range(2)]
        turn = [region[0][:, 0:512], region[0][:, 512:1024], region[1][:, 0:512], region[1][:, 512:1024]]

        in_const = sem("in_const")
        in_tokw = sem("in_tokw")
        in_x = [[sem(f"in_x{l}{c}") for c in range(CHANNELS)] for l in range(2)]
        x_sorted = sem("x_sorted")
        in_attnw = sem("in_attnw")
        in_rest = sem("in_rest")
        in_tab = [sem(f"in_tab{j}") for j in range(4)]
        pool_ready = sem("pool_ready")
        turned = sem("turned")
        turned_by_act = sem("turned_by_act")
        turned_by_dve = sem("turned_by_dve")
        pos_biased = sem("pos_biased")
        pos_turned = sem("pos_turned")
        posT_ready = sem("posT_ready")
        keys_turned = sem("keys_turned")
        keysB_ready = sem("keysB_ready")
        embedded = sem("embedded")
        h0T_ready = sem("h0T_ready")
        h0s_ready = sem("h0s_ready")
        kv_done = sem("kv_done")
        kv_ready = sem("kv_ready")
        h0x2_ready = sem("h0x2_ready")
        scored = sem("scored")
        max_ready = sem("max_ready")
        probs_ready = sem("probs_ready")
        probs_turned = sem("probs_turned")
        probsT_ready = sem("probsT_ready")
        attended = sem("attended")
        var_ready = sem("var_ready")
        rstd_ready = sem("rstd_ready")
        h1s_ready = sem("h1s_ready")
        h1_ready = sem("h1_ready")
        h1_turned = sem("h1_turned")
        h1T_ready = sem("h1T_ready")
        query_done = sem("query_done")
        qs_ready = sem("qs_ready")
        sim_done = sem("sim_done")
        sims_read = sem("sims_read")
        tab_turned = sem("tab_turned")
        dT_hi_ready = sem("dT_hi_ready")
        dT_lo_ready = sem("dT_lo_ready")
        h1T_hi_ready = sem("h1T_hi_ready")
        h1T_lo_ready = sem("h1T_lo_ready")
        up_hi_ready = sem("up_hi_ready")
        up_lo_ready = sem("up_lo_ready")
        G_hi_ready = sem("G_hi_ready")
        G_lo_ready = sem("G_lo_ready")
        G_free = sem("G_free")
        dots_done = sem("dots_done")
        S_ready = sem("S_ready")
        diffs_ready = sem("diffs_ready")
        exps_ready = sem("exps_ready")
        gates_done = sem("gates_done")
        gate_ready = sem("gate_ready")
        hidden_free = sem("hidden_free")
        onehots_ready = sem("onehots_ready")
        region_done = sem("region_done")
        region_free = sem("region_free")
        chunk_used = sem("chunk_used")
        summed = sem("summed")
        outT_ready = sem("outT_ready")
        out_turned = sem("out_turned")
        var2_ready = sem("var2_ready")
        rstd2_ready = sem("rstd2_ready")
        result_ready = sem("result_ready")
        stored = [sem(f"stored{r}") for r in range(4)]
        dve_step = sem("dve_step")

        block = ctx.enter_context(nc.Block())

        MEAN, VAR, VAR_EPS, RSTD, NEG_MAX, SUM, RECIP, STATS = range(8)

        def stat(u, n, cols=1):
            return small[:, 16 * u + n:16 * u + n + cols]

        def blocks_of(nat, rows, k):
            return [nat[:, o, k * P:(k + 1) * P] for o in range(rows)]

        def x_blocks(l, k):
            c, i = divmod(k, 2)
            return [x_feats[:, c, l, w, i * P:(i + 1) * P] for w in range(GRID)]

        def two(dst, k):
            return dst[:, k:k + 2, :].rearrange("p k o -> p (k o)")

        in_rest_all = 7 * 16
        groups = [("tokw", [b for k in (g, g + 1) for b in blocks_of(tokw_nat, DK, k)], two(tokwT, g), in_tokw, 16)
                  for g in range(0, FK, 2)]
        groups += [("x0", x_blocks(0, k), xT[:, 0, k, :], x_sorted, k // 2 + 1) for k in range(FK)]
        groups += [("x1", x_blocks(1, k), xT[:, 1, k, :], x_sorted, CHANNELS + k // 2 + 1) for k in range(FK)]
        groups += [("attnw", blocks_of(attnw_nat, 2 * DK, k), attnwT[:, k, :], in_attnw, 16) for k in range(DK)]
        groups += [("queryw", [b for k in range(DK) for b in blocks_of(queryw_nat, DK, k)], querywT_flat,
                    in_rest, in_rest_all)]
        groups += [("gatew", blocks_of(gatew_nat, MK, k), gatewT[:, k, :], in_rest, in_rest_all) for k in range(DK)]
        groups += [("upw", blocks_of(upw_nat, MK, k), upwT[:, k, :], in_rest, in_rest_all) for k in range(DK)]
        groups += [("downw", [b for k in (g, g + 1) for b in blocks_of(downw_nat, DK, k)], two(downwT, g),
                    in_rest, in_rest_all) for g in range(0, MK, 2)]
        names = [g[0] for g in groups]
        n_groups = len(groups)
        x1_starts, weights_start = names.index("x1"), names.index("attnw")

        def act_groups(g):
            return (g + 1) // 2

        sums = [[bank[2][:, :], bank[3][:, :]], [bank[0][:, :], bank[1][:, :]]]
        gate_out = dT[:, :, :, :].rearrange("p u k t -> p (u k t)")
        down_rows = down_embed.rearrange("(c p) d -> p c d", p=P)
        up_rows = up_embed.rearrange("(c p) d -> p c d", p=P)

        def out_slot(t):
            return [bank[2][:, 0:D], bank[3][:, 0:D], region[0][:, 0:D], region[0][:, 512:512 + D]][t % 4]

        @block.sync
        def _(sp):
            sp.dma_start(ident[:, :], constants[:, 0:P]).then_inc(in_const, 16)
            sp.dma_start(slot_mask[:, :], constants[:, 2 * P:2 * P + 2]).then_inc(in_const, 16)
            sp.dma_start(pos_nat[0:PATCHES, :], pos_emb).then_inc(in_const, 16)
            sp.dma_start(bias_rows[0:PATCHES, :], tok_b.partition_broadcast(PATCHES)).then_inc(in_const, 16)
            sp.dma_start(tokw_nat, tok_w.rearrange("(o p) f -> p o f", p=P)).then_inc(in_tokw, 16)
            image_rows = x.rearrange("b c (q l i) w -> q l b c i w", q=2, l=2, i=PATCH)
            for l in range(2):
                for c in range(CHANNELS):
                    for q in range(2):
                        sp.dma_start(x_rows[64 * q:64 * q + 64, c, l, :].rearrange("p (i w) -> p i w", w=SIDE),
                                     image_rows[q, l, :, c, :, :]).then_inc(in_x[l][c], 16)
            sp.dma_start(attnw_nat, attn_w.rearrange("(o p) f -> p o f", p=P)).then_inc(in_attnw, 16)
            sp.dma_start(queryw_nat, w_queries.rearrange("(o p) f -> p o f", p=P)).then_inc(in_rest, 16)
            sp.dma_start(gatew_nat, w_gate.rearrange("(o p) f -> p o f", p=P)).then_inc(in_rest, 16)
            sp.dma_start(upw_nat, w_up.rearrange("(o p) f -> p o f", p=P)).then_inc(in_rest, 16)
            sp.dma_start(downw_nat, w_down.rearrange("(o p) f -> p o f", p=P)).then_inc(in_rest, 16)
            for s in range(2):
                sp.dma_start(keys_nat[:, s, :].rearrange("p (h n) -> p h n", h=HEADS),
                             keys.rearrange("h k s n -> s k h n")[s]).then_inc(in_rest, 16)
            sp.dma_start(mask, constants[:, P:2 * P]).then_inc(in_rest, 16)
            for j in range(4):
                sp.dma_start(tab[:, j, :], down_rows[:, j, :]).then_inc(in_tab[j], 16)
            with sp.Fori(1, TILES) as i:
                for j in range(4):
                    sp.wait_ge(tab_turned, i * 4 + (j - 3))
                    sp.dma_start(tab[:, j, :], down_rows[:, ds(i * 4 + j, 1), :].rearrange("p c d -> p (c d)")
                                 ).then_inc(in_tab[j], 16)
            for j in range(4):
                sp.wait_ge(tab_turned, CHUNKS - 3 + j)
                sp.dma_start(tab[:, j, :], up_rows[:, j, :]).then_inc(in_tab[j], 16)
            with sp.Fori(1, TILES) as i:
                for j in range(4):
                    sp.wait_ge(chunk_used, i * 4 + (j - 3))
                    sp.dma_start(tab[:, j, :], up_rows[:, ds(i * 4 + j, 1), :].rearrange("p c d -> p (c d)")
                                 ).then_inc(in_tab[j], 16)
            for j in range(4):
                sp.wait_ge(chunk_used, CHUNKS - 3 + j)
                sp.dma_start(tab[:, j, :], up_rows[:, j, :]).then_inc(in_tab[j], 16)
            with sp.Fori(1, TILES) as i:
                for j in range(4):
                    sp.wait_ge(up_lo_ready, i * 4 + (j - 3))
                    sp.dma_start(tab[:, j, :], up_rows[:, ds(i * 4 + j, 1), :].rearrange("p c d -> p (c d)")
                                 ).then_inc(in_tab[j], 16)
            out_rows = out.rearrange("b n d -> (b n) d")
            for t in range(TILES):
                sp.wait_ge(result_ready, t + 1)
                sp.dma_start(out_rows[t * P:(t + 1) * P, :], result[:, t % 4, :]).then_inc(stored[t % 4], 16)
            for r in range(4):
                sp.wait_ge(stored[r], 16 * TILES // 4)

        @block.gpsimd
        def _(pool):
            pool.memset(keysB, 0.0).then_inc(pool_ready, 1)
            pool.memset(minus_half[:, :], -0.5).then_inc(pool_ready, 1)
            pool.iota(iota8[:, :], [[1, TOPK]], base=0, channel_multiplier=0,
                      allow_small_or_imprecise_dtypes=True).then_inc(pool_ready, 1)
            pool.iota(grid[:, :, :], [[1, KEYS], [0, STEP]], base=0, channel_multiplier=0,
                      allow_small_or_imprecise_dtypes=True).then_inc(pool_ready, 1)
            for l in range(2):
                for c in range(CHANNELS):
                    pool.wait_ge(in_x[l][c], 32)
                    pool.tensor_copy(x_feats[:, c, l, :, :].rearrange("p w (i j) -> p w i j", j=PATCH),
                                     x_rows[:, c, l, :].rearrange("p (i w j) -> p w i j", w=GRID, j=PATCH)
                                     ).then_inc(x_sorted, 1)
            pool.wait_ge(h0T_ready, 4)
            for u in range(2):
                pool.tensor_copy(h0s[:, u, :, :], h0T[:, :, u * P:(u + 1) * P]).then_inc(h0s_ready, 1)
            pool.wait_ge(pool_ready, 4)
            with pool.Fori(0, TILES // 2) as i:
                for u in range(2):
                    pool.wait_ge(scored, i * 2 + (u + 1))
                    following = (i * 2 + (u + 2)) % TILES
                    pool.tensor_copy(h0s[:, u, :, :], h0T[:, :, ds(following * P, P)]).then_inc(h0s_ready, 1)
                for u in range(2):
                    pool.wait_ge(var_ready, i * 2 + (u + 1))
                    pool.tensor_tensor(stat(u, RSTD), stat(u, VAR_EPS), minus_half[:, :],
                                       ALU.pow).then_inc(rstd_ready, 1)
                for u in range(2):
                    pool.wait_ge(h1s_ready, i * 2 + (u + 1))
                    pool.tensor_copy(h1[:, ds(i * 2 + u, 1), :].rearrange("p t d -> p (t d)"), h1s[:, u, :]
                                     ).then_inc(h1_ready, 1)
                for u in range(2):
                    pool.wait_ge(h1T_hi_ready, i * 2 + (u + 1))
                    cols = ds((i * 2 + u) * P, P)
                    pool.tensor_tensor(h1T_lo[:, :, cols], h1T[:, :, cols], h1T_hi[:, :, cols].bitcast(F32),
                                       ALU.subtract).then_inc(h1T_lo_ready, 1)
            with pool.Fori(0, TILES) as i:
                for j in range(4):
                    pool.wait_ge(dT_hi_ready, i * 4 + (j + 1))
                    pool.tensor_tensor(dT_lo[:, j % 2, :, :], dT[:, j % 2, :, :], dT_hi[:, j % 2, :, :].bitcast(F32),
                                       ALU.subtract).then_inc(dT_lo_ready, 1)
            def split_up(first, end):
                with pool.Fori(first, end) as i:
                    for j in range(4):
                        pool.wait_ge(up_hi_ready, i * 4 + (j + 1))
                        pool.tensor_tensor(up_lo[:, j, :], tab[:, j, :], up_hi[:, j, :].bitcast(F32),
                                           ALU.subtract).then_inc(up_lo_ready, 1)

            for t in range(TILES):
                if t < TILES // 2:
                    split_up(2 * t, 2 * t + 2)
                pool.wait_ge(var2_ready, t + 1)
                pool.tensor_tensor(stat(t % 2, RSTD), stat(t % 2, VAR_EPS), minus_half[:, :],
                                   ALU.pow).then_inc(rstd2_ready, 1)

        @block.tensor
        def _(pe):
            def turn_group(g):
                _, blocks, _, arrived, value = groups[g]
                pe.wait_ge(arrived, value)
                if g >= 4 and g % 2 == 0:
                    pe.wait_ge(turned_by_act, (g - 4) // 2 + 1)
                elif g >= 4:
                    pe.wait_ge(turned_by_dve, (g - 4) // 2 + 1)
                for n, b in enumerate(blocks):
                    last = pe.transpose(turn[g % 4][:, n * P:(n + 1) * P], b, ident[:, :])
                last.then_inc(turned, 1)

            def embed(l, groups_before):
                pe.wait_ge(turned_by_act, act_groups(groups_before))
                pe.wait_ge(turned_by_dve, groups_before - act_groups(groups_before))
                for o in range(DK):
                    for k in range(FK):
                        last = pe.matmul(bank[2 * l + o][:, :], tokwT[:, k, o * P:(o + 1) * P], xT[:, l, k, :],
                                         start=(k == 0), stop=(k == FK - 1))
                    last.then_inc(embedded, 1)

            pe.wait_ge(in_const, 64)
            pe.wait_ge(pos_biased, 1)
            for k in range(DK):
                last = pe.transpose(bank[3][:, k * PATCHES:(k + 1) * PATCHES],
                                    pos_nat[0:PATCHES, k * P:(k + 1) * P], ident[0:PATCHES, 0:PATCHES])
            last.then_inc(pos_turned, 1)
            for g in range(x1_starts):
                turn_group(g)
            embed(0, x1_starts)
            for g in range(x1_starts, weights_start):
                turn_group(g)
            pe.wait_ge(posT_ready, 1)
            embed(1, weights_start)
            for g in range(weights_start, n_groups):
                turn_group(g)
            pe.wait_ge(turned_by_act, act_groups(n_groups))
            pe.wait_ge(turned_by_dve, n_groups - act_groups(n_groups))
            for s in range(2):
                last = pe.transpose(turn[0][:, s * P:(s + 1) * P], keys_nat[:, s, :], ident[:, :])
            last.then_inc(keys_turned, 1)

            pe.wait_ge(keysB_ready, 4)
            pe.wait_ge(h0T_ready, 4)
            with pe.Fori(0, TILES // 2) as i:
                for u in range(2):
                    pe.wait_ge(h0s_ready, i * 2 + (u + 1))
                    for o in range(DK):
                        for k in range(DK):
                            pe.matmul(bank[u][:, o * P:(o + 1) * P], attnwT[:, k, o * P:(o + 1) * P],
                                      h0s[:, u, k, :], start=(k == 0), stop=(k == DK - 1))
                    for k in range(DK):
                        last = pe.matmul(bank[u][:, D:2 * D], h0s[:, u, k, :], attnwT[:, k, D:2 * D],
                                         start=(k == 0), stop=(k == DK - 1))
                    last.then_inc(kv_done, 1)
                    for k in range(DK):
                        last = pe.transpose(region[u][:, k * P:(k + 1) * P], h0s[:, u, k, :], ident[:, :])
                    last.then_inc(kv_done, 1)
                for u in range(2):
                    pe.wait_ge(kv_ready, i * 2 + (u + 1))
                    pe.wait_ge(h0x2_ready, i * 2 + (u + 1))
                    for k in range(DK):
                        last = pe.matmul(region[u][:, 256:384], h0s[:, u, k, :], kv[:, u, k * P:(k + 1) * P],
                                         start=(k == 0), stop=(k == DK - 1))
                    last.then_inc(scored, 1)
                for u in range(2):
                    pe.wait_ge(probs_ready, i * 2 + (u + 1))
                    pe.transpose(region[u][:, 384:512], probs[:, u, :], ident[:, :]).then_inc(probs_turned, 1)
                for u in range(2):
                    pe.wait_ge(probsT_ready, i * 2 + (u + 1))
                    pe.matmul(region[u][:, 512:768], probsT[:, u, :], kv[:, u, D:2 * D],
                              start=True, stop=True).then_inc(attended, 1)
                for u in range(2):
                    pe.wait_ge(h1s_ready, i * 2 + (u + 1))
                    for k in range(DK):
                        last = pe.transpose(region[u][:, 768 + k * P:768 + (k + 1) * P],
                                            h1s[:, u, k * P:(k + 1) * P], ident[:, :])
                    last.then_inc(h1_turned, 1)

            pe.wait_ge(h1T_lo_ready, TILES)

            def turn_chunk(i, j):
                pe.wait_ge(in_tab[j], i * 16 + 16)
                for k in range(DK):
                    last = pe.transpose(bank[j % 2][:, k * P:(k + 1) * P],
                                        tab[:, j, k * P:(k + 1) * P], ident[:, :])
                last.then_inc(tab_turned, 1)

            def dots(i, j):
                pe.wait_ge(dT_lo_ready, i * 4 + (j + 1))
                for half in range(2):
                    pe.wait_ge(S_ready, i * 8 + (2 * j + half + 1))
                    parts = ((dT_hi, h1T_hi), (dT_hi, h1T_lo), (dT_lo, h1T_hi))
                    for k in range(DK):
                        for n, (a, b) in enumerate(parts):
                            last = pe.matmul(bank[2 + half][:, :], a[:, j % 2, k, :],
                                             b[:, k, half * HALF:(half + 1) * HALF],
                                             start=(k == 0 and n == 0), stop=(k == DK - 1 and n == 2))
                    last.then_inc(dots_done, 1)

            def look_up(i, is_last):
                for s in range(2):
                    for k in range(DK):
                        last = pe.matmul(region[1][:, s * P:(s + 1) * P], querywT[:, k, s * P:(s + 1) * P],
                                         h1T[:, k, ds(i * P, P)], start=(k == 0), stop=(k == DK - 1))
                last.then_inc(query_done, 1)
                turn_chunk(i, 1)
                dots(i, 0)
                pe.wait_ge(qs_ready, i + 1)
                for s in range(2):
                    last = pe.matmul(region[0][:, s * 512:(s + 1) * 512], qs[:, s, :], keysB[:, s, :],
                                     start=True, stop=True)
                last.then_inc(sim_done, 1)
                turn_chunk(i, 2)
                dots(i, 1)
                turn_chunk(i, 3)
                dots(i, 2)
                if not is_last:
                    turn_chunk(i + 1, 0)
                dots(i, 3)
                pe.wait_ge(sims_read, i + 1)

            turn_chunk(0, 0)
            with pe.Fori(0, TILES - 1) as i:
                look_up(i, False)
            look_up(TILES - 1, True)

            def build_C(n, parity):
                pe.wait_ge(onehots_ready, n + 1)
                for g in range(2):
                    pe.wait_ge(region_free, n * 2 + (g + 1))
                    for s in range(STEP):
                        for part in range(2):
                            last = pe.matmul(region[g][:, s * 64:(s + 1) * 64],
                                             onehot_y[64 * g:64 * g + 64, parity, :, s],
                                             weighted_x[64 * g:64 * g + 64, parity, 2 * part:2 * part + 2, :, s],
                                             start=(part == 0), stop=(part == 1))
                    last.then_inc(region_done, 1)

            pe.wait_ge(S_ready, 2 * CHUNKS + 2)
            with pe.Fori(0, 2) as half:
                for q in range(MK):
                    for b, w in ((0, gatewT), (1, upwT)):
                        pe.wait_ge(hidden_free, half * MK + (q + 1))
                        for k in range(DK):
                            last = pe.matmul(bank[b][:, :], w[:, k, q * P:(q + 1) * P],
                                             h1T[:, k, ds(half * HALF, HALF)], start=(k == 0), stop=(k == DK - 1))
                        last.then_inc(gates_done, 1)
                    build_C(half * MK + q, q % 2)

            def add_mlp(half, blocks):
                for fk in blocks:
                    for o in range(DK):
                        last = pe.matmul(sums[half][o], downwT[:, fk, o * P:(o + 1) * P],
                                         mT[:, fk, half * HALF:(half + 1) * HALF],
                                         start=(fk == 0), stop=(fk == MK - 1), skip_group_check=True)
                return last

            def add_split_chunks(half, i):
                for j in range(4):
                    pe.wait_ge(up_lo_ready, i * 4 + (j + 1))
                    pe.wait_ge(G_lo_ready, i * 4 + (j + 1))
                    for o in range(DK):
                        for a, b in ((up_hi, G_hi), (up_hi, G_lo), (up_lo, G_hi)):
                            last = pe.matmul(sums[half][o], a[:, j, o * P:(o + 1) * P], b[:, j, :],
                                             start=False, stop=False, skip_group_check=True)
                    last.then_inc(G_free, 1)

            def add_chunks(half, i, base):
                for j in range(4):
                    pe.wait_ge(in_tab[j], base)
                    for o in range(DK):
                        last = pe.matmul(sums[half][o], tab[:, j, o * P:(o + 1) * P],
                                         S[:, ds(i * 4 + j, 1), half * HALF:(half + 1) * HALF]
                                         .rearrange("p c t -> p (c t)"),
                                         start=False, stop=False, skip_group_check=True)
                    last.then_inc(chunk_used, 1)

            def turn_output(half):
                pe.wait_ge(outT_ready, DK * (half + 1))
                if half:
                    pe.wait_ge(result_ready, TILES // 2)
                for t in range(TILES // 2 * half, TILES // 2 * (half + 1)):
                    a = t % (TILES // 2) * P
                    for o in range(DK):
                        last = pe.transpose(out_slot(t)[:, o * P:(o + 1) * P], outT[:, o, a:a + P], ident[:, :])
                    last.then_inc(out_turned, 1)

            pe.wait_ge(hidden_free, 2 * MK + 1)
            add_mlp(0, (0, 1))
            pe.wait_ge(region_free, HALF_TILES + 2)
            with pe.Fori(0, TILES // 2) as i:
                for q in range(2):
                    add_chunks(0, i * 2 + q, i * 32 + 16 * (TILES + q + 1))
                    build_C(i * 2 + (HALF_TILES // 2 + q), q)
            add_mlp(0, (2, 3)).then_inc(summed, 1)
            pe.sem_inc(G_free, 4)
            add_mlp(1, (0, 1))
            pe.wait_ge(region_free, 2 * HALF_TILES + 2)
            turn_output(0)
            with pe.Fori(0, TILES) as i:
                add_split_chunks(1, i)
            add_mlp(1, (2, 3)).then_inc(summed, 1)
            turn_output(1)

        @block.scalar
        def _(act):
            for g in range(0, n_groups, 2):
                act.wait_ge(turned, g + 1)
                if names[g] == "queryw":
                    act.wait_ge(pool_ready, 1)
                act.copy(groups[g][2], turn[g % 4]).then_inc(turned_by_act, 1)
            act.wait_ge(keys_turned, 1)
            act.wait_ge(pool_ready, 1)
            for h in range(HEADS):
                act.copy(keysB[RET * h:RET * (h + 1), :, h * KEYS:(h + 1) * KEYS],
                         turn[0][RET * h:RET * (h + 1), 0:256].rearrange("p (s k) -> p s k", s=2)
                         ).then_inc(keysB_ready, 1)

            with act.Fori(0, TILES // 2) as i:
                for u in range(2):
                    act.wait_ge(kv_done, i * 4 + (2 * u + 1))
                    act.copy(kv[:, u, :], bank[u][:, :]).then_inc(kv_ready, 1)
                    act.wait_ge(kv_done, i * 4 + (2 * u + 2))
                    act.mul(h0x2[:, u, :], region[u][:, 0:256], 2.0).then_inc(h0x2_ready, 1)
                for u in range(2):
                    act.wait_ge(max_ready, i * 2 + (u + 1))
                    act.activation(probs[:, u, :], masked[:, u, :], ACT.Exp, bias=stat(u, NEG_MAX),
                                   accum_out=stat(u, SUM)).then_inc(probs_ready, 1)
                for u in range(2):
                    act.wait_ge(probs_turned, i * 2 + (u + 1))
                    act.copy(probsT[:, u, :], region[u][:, 384:512]).then_inc(probsT_ready, 1)
                for u in range(2):
                    act.wait_ge(h1_turned, i * 2 + (u + 1))
                    act.copy(h1T[:, :, ds((i * 2 + u) * P, P)],
                             region[u][:, 768:1024].rearrange("p (k t) -> p k t", k=DK)).then_inc(h1T_ready, 1)
                    act.wait_ge(h1T_ready, i * 2 + (u + 1))
                    act.copy(h1T_hi[:, :, ds((i * 2 + u) * P, P)], h1T[:, :, ds((i * 2 + u) * P, P)]
                             ).then_inc(h1T_hi_ready, 1)

            act.wait_ge(h0s_ready, TILES + 2)
            act.sem_inc(S_ready, 2)
            act.activation(held[:, 1:2], minus_half[:, :], ACT.Silu)

            def chunk_out(i, j):
                act.wait_ge(tab_turned, i * 4 + (j + 1))
                turned_chunk = bank[j % 2][:, 0:256].rearrange("p (k t) -> p k t", k=DK)
                act.copy(dT[:, j % 2, :, :], turned_chunk)
                act.copy(dT_hi[:, j % 2, :, :], turned_chunk).then_inc(dT_hi_ready, 1)

            def silu(i, j):
                for half in range(2):
                    act.wait_ge(dots_done, i * 8 + (2 * j + half + 1))
                    act.activation(S[:, ds(i * 4 + j, 1), half * HALF:(half + 1) * HALF]
                                   .rearrange("p c t -> p (c t)"), bank[2 + half][:, :], ACT.Silu
                                   ).then_inc(S_ready, 1)

            def look_up(i, is_last):
                act.wait_ge(query_done, i + 1)
                act.copy(qs, region[1][:, 0:256].rearrange("p (s t) -> p s t", s=2)).then_inc(qs_ready, 1)
                chunk_out(i, 1)
                silu(i, 0)
                chunk_out(i, 2)
                silu(i, 1)
                chunk_out(i, 3)
                silu(i, 2)
                if not is_last:
                    chunk_out(i + 1, 0)
                silu(i, 3)

            chunk_out(0, 0)
            with act.Fori(0, TILES - 1) as i:
                look_up(i, False)
            look_up(TILES - 1, True)
            act.wait_ge(diffs_ready, TILES)
            act.activation(exps, diffs, ACT.Exp).then_inc(exps_ready, 1)
            act.activation(held[:, 1:2], minus_half[:, :], ACT.Silu)

            with act.Fori(0, 2) as half:
                for q in range(MK):
                    act.wait_ge(gates_done, half * (2 * MK) + (2 * q + 1))
                    act.wait_ge(hidden_free, half * MK + (q + 1))
                    act.activation(gate_out, bank[0][:, :], ACT.Silu).then_inc(gate_ready, 1)

            def split_chunks():
                act.wait_ge(region_free, 2 * HALF_TILES + 2)
                act.wait_ge(hidden_free, 2 * MK + 1)
                with act.Fori(0, TILES) as i:
                    for j in range(4):
                        act.wait_ge(G_free, i * 4 + (j + 1))
                        act.wait_ge(in_tab[j], i * 16 + 16 * (2 * TILES + 1))
                        act.copy(up_hi[:, j, :], tab[:, j, :]).then_inc(up_hi_ready, 1)
                        act.copy(G_hi[:, j, :], S[:, ds(i * 4 + j, 1), HALF:2 * HALF]
                                 .rearrange("p c t -> p (c t)")).then_inc(G_hi_ready, 1)

            for half in range(2):
                if half:
                    split_chunks()
                act.wait_ge(summed, half + 1)
                if half:
                    act.wait_ge(out_turned, TILES // 2)
                for o in range(DK):
                    act.mul(outT[:, o, :], sums[half][o], 1.0 / WSCALE).then_inc(outT_ready, 1)

        @block.vector
        def _(dve):
            steps = [0]

            def step(ins):
                steps[0] += 1
                ins.then_inc(dve_step, 1)
                dve.wait_ge(dve_step, steps[0])

            def hold():
                dve.memset(held[:, 0:1], 0.0)

            def embed_out(l):
                for o in range(DK):
                    dve.wait_ge(embedded, 2 * l + o + 1)
                    dve.tensor_tensor(
                        h0T[:, o, :].rearrange("p (b q l w) -> p l w q b", q=2, l=2, w=GRID)[:, l],
                        bank[2 * l + o][:, :].rearrange("p (w q b) -> p w q b", w=GRID, q=2),
                        posT[:, o, :].rearrange("p (q l w) -> p l w q", q=2, l=2)[:, l].unsqueeze(3)
                        .broadcast_to([P, GRID, 2, IMAGES]), ALU.add).then_inc(h0T_ready, 1)

            def take_out(first, end):
                for g in range(first + (first + 1) % 2, end, 2):
                    dve.wait_ge(turned, g + 1)
                    dve.tensor_copy(groups[g][2], turn[g % 4]).then_inc(turned_by_dve, 1)

            dve.wait_ge(in_const, 64)
            dve.tensor_tensor(pos_nat[0:PATCHES, :], pos_nat[0:PATCHES, :], bias_rows[0:PATCHES, :], ALU.add
                              ).then_inc(pos_biased, 1)
            dve.wait_ge(pos_turned, 1)
            dve.tensor_copy(posT, bank[3][:, 0:DK * PATCHES].rearrange("p (k n) -> p k n", k=DK)
                            ).then_inc(posT_ready, 1)
            dve.wait_ge(posT_ready, 1)
            take_out(0, x1_starts)
            embed_out(0)
            take_out(x1_starts, weights_start)
            embed_out(1)
            take_out(weights_start, n_groups)

            dve.sem_inc(hidden_free, 1)
            dve.sem_inc(region_free, 2)

            dve.wait_ge(in_rest, in_rest_all)
            loop_base = steps[0]
            per_turn = 2 * 5
            with dve.Fori(0, TILES // 2) as i:
                n = [0]

                def chain(ins):
                    n[0] += 1
                    ins.then_inc(dve_step, 1)
                    dve.wait_ge(dve_step, i * per_turn + (loop_base + n[0]))

                for u in range(2):
                    dve.wait_ge(scored, i * 2 + (u + 1))
                    chain(dve.tensor_tensor(masked[:, u, :], region[u][:, 256:384], mask, ALU.add))
                    dve.tensor_reduce(stat(u, NEG_MAX), masked[:, u, :], AX_X, ALU.max, negate=True
                                      ).then_inc(max_ready, 1)
                for u in range(2):
                    dve.wait_ge(probs_ready, i * 2 + (u + 1))
                    dve.wait_ge(h0x2_ready, i * 2 + (u + 1))
                    chain(dve.reciprocal(stat(u, RECIP), stat(u, SUM)))
                    dve.wait_ge(attended, i * 2 + (u + 1))
                    chain(dve.scalar_tensor_tensor(y1[:, u, :], region[u][:, 512:768], stat(u, RECIP),
                                                   h0x2[:, u, :], ALU.mult, ALU.add))
                    chain(dve.bn_stats(stat(u, STATS, 6), y1[:, u, :]))
                    hold()
                    chain(dve.bn_aggr(stat(u, MEAN, 2), stat(u, STATS, 6)))
                    dve.tensor_scalar(stat(u, VAR_EPS), stat(u, VAR), EPS, None, ALU.add).then_inc(var_ready, 1)
                for u in range(2):
                    dve.wait_ge(rstd_ready, i * 2 + (u + 1))
                    dve.tensor_scalar(h1s[:, u, :], y1[:, u, :], stat(u, MEAN), stat(u, RSTD),
                                      ALU.subtract, ALU.mult).then_inc(h1s_ready, 1)
                assert n[0] == per_turn
            steps[0] += per_turn * (TILES // 2)

            loop_base2 = steps[0]
            per_tile = 10
            dve.wait_ge(pool_ready, 4)
            with dve.Fori(0, TILES) as i:
                n = [0]

                def chain(ins):
                    n[0] += 1
                    ins.then_inc(dve_step, 1)
                    dve.wait_ge(dve_step, i * per_tile + (loop_base2 + n[0]))

                def sims(s, h):
                    return region[0][:, s * 512 + h * KEYS:s * 512 + (h + 1) * KEYS]

                pairs = [(s, h) for s in range(2) for h in range(HEADS)]
                dve.wait_ge(sim_done, i + 1)
                hold()
                for s, h in pairs:
                    last = dve.max(top_val[:, s, h, :], sims(s, h))
                chain(last)
                hold()
                for s, h in pairs:
                    last = dve.max_index(top_idx[:, s, h, :], top_val[:, s, h, :], sims(s, h))
                last.then_inc(sims_read, 1)
                chain(dve.tensor_tensor(
                    pair_sum.rearrange("p (h i j) -> p h i j", h=HEADS, i=TOPK),
                    top_val[:, 0].unsqueeze(3).broadcast_to([P, HEADS, TOPK, TOPK]),
                    top_val[:, 1].unsqueeze(2).broadcast_to([P, HEADS, TOPK, TOPK]), ALU.add))
                hold()
                for h in range(HEADS):
                    last = dve.max(pair_val[:, h, :], pair_sum[:, h * 64:(h + 1) * 64])
                chain(last)
                hold()
                for h in range(HEADS):
                    last = dve.max_index(pair_pos[:, h * TOPK:(h + 1) * TOPK], pair_val[:, h, :],
                                         pair_sum[:, h * 64:(h + 1) * 64])
                chain(last)
                dve.tensor_scalar(pair_ij[:, 0, :], pair_pos[:, :], 3, None, ALU.logical_shift_right)
                chain(dve.tensor_scalar(pair_ij[:, 1, :], pair_pos[:, :], TOPK - 1, None, ALU.bitwise_and))
                chain(dve.tensor_tensor(
                    match, pair_ij[:, :, :].rearrange("p s a -> p (s a)").unsqueeze(2)
                    .broadcast_to([P, 2 * PICKS, TOPK]),
                    iota8[:, :].unsqueeze(1).broadcast_to([P, 2 * PICKS, TOPK]), ALU.is_equal))
                dve.wait_ge(sims_read, i + 1)
                chain(dve.tensor_tensor(
                    match.rearrange("p (g k) i -> p g k i", k=TOPK),
                    match.rearrange("p (g k) i -> p g k i", k=TOPK),
                    top_idx[:, :, :, :].rearrange("p s h i -> p (s h) i").unsqueeze(2)
                    .broadcast_to([P, 2 * HEADS, TOPK, TOPK]), ALU.mult))
                chain(dve.tensor_reduce(row_xy[:, :, :].rearrange("p s a -> p (s a)"), match, AX_X, ALU.add))
                chain(dve.tensor_scalar(edge[:, :], row_xy[:, 0, :], float(CHUNKS), float(KEYS - 1),
                                        ALU.is_ge, ALU.mult))
                dve.tensor_scalar(pack[:, ds(i, 1), 0, :].rearrange("p t a -> p (t a)"), row_xy[:, 0, :],
                                  float(CHUNKS - 1), None, ALU.min)
                chain(dve.tensor_tensor(pack[:, ds(i, 1), 1, :].rearrange("p t a -> p (t a)"), row_xy[:, 1, :],
                                        edge[:, :], ALU.max))
                dve.tensor_tensor(diffs[:, ds(i, 1), :].rearrange("p t (h k) -> p (t h) k", h=HEADS), pair_val[:, :, :],
                                  pair_val[:, :, 0:1].broadcast_to([P, HEADS, TOPK]), ALU.subtract
                                  ).then_inc(diffs_ready, 1)
                assert n[0] == per_tile, n[0]
            steps[0] += per_tile * TILES

            heads = "p t (h k) -> p (t h) k"
            sums8 = top_val[:, :, :, :].rearrange("p s h k -> p (s h k)")[:, 0:32]
            recips = top_val[:, :, :, :].rearrange("p s h k -> p (s h k)")[:, 32:64]
            dve.wait_ge(exps_ready, 1)
            step(dve.tensor_reduce(sums8, exps.rearrange(heads, h=HEADS), AX_X, ALU.add))
            step(dve.reciprocal(recips, sums8))
            step(dve.scalar_tensor_tensor(diffs.rearrange(heads, h=HEADS), exps.rearrange(heads, h=HEADS), WSCALE,
                                          recips.unsqueeze(2).broadcast_to([P, TILES * HEADS, TOPK]),
                                          ALU.mult, ALU.mult))
            step(dve.tensor_copy(pack[:, :, 2, :], diffs))
            step(dve.tensor_tensor(pack[:, :, 3, :], diffs, pack[:, :, 2, :], ALU.subtract))
            step(dve.transpose(selT[:, :, :, :].rearrange("p t q s -> p (t q s)"),
                               pack.rearrange("p t q a -> p (t q a)")))
            for slot in range(2):
                last = dve.tensor_scalar(selW[:, :, :, slot, :], selT[:, :, 2:4, :], slot_mask[:, slot:slot + 1],
                                         None, ALU.mult)
            step(last)

            def onehots(tile, hf, x_done):
                cols = slice(STEP * hf, STEP * (hf + 1))
                dve.tensor_tensor(onehot_x[:, hf, :, :], grid[:, 0:32, :],
                                  selT[:, tile, 0, cols].broadcast_to([P, 32, STEP]), ALU.is_equal
                                  ).then_inc(dve_step, 1)
                dve.tensor_tensor(onehot_y[:, hf, :, :], grid[:, :, :],
                                  selT[:, tile, 1, cols].broadcast_to([P, KEYS, STEP]), ALU.is_equal)
                dve.wait_ge(dve_step, x_done)
                dve.tensor_tensor(weighted_x[:, hf, :, :, :],
                                  onehot_x[:, hf:hf + 1, :, :].broadcast_to([P, 4, 32, STEP]),
                                  selW[:, tile, :, :, cols].rearrange("p t a b s -> p (t a b) s").unsqueeze(2)
                                  .broadcast_to([P, 4, 32, STEP]), ALU.mult).then_inc(onehots_ready, 1)

            S_tiles = S[:, :, :].rearrange("p x (n b t) -> p x n b t", n=TILES, b=4)

            def multiply(tile, hf, n):
                for g in range(2):
                    dve.wait_ge(region_done, n * 2 + (g + 1))
                    block_S = S_tiles[:, :, tile, 2 * g:2 * g + 2, STEP * hf:STEP * (hf + 1)].rearrange(
                        "p x n b t -> p x (n b) t")
                    dve.tensor_tensor(block_S, region[g][:, :].rearrange("p (s b x) -> p x b s", s=STEP, b=2),
                                      block_S, ALU.mult).then_inc(region_free, 1)

            def one(tile):
                return slice(tile, tile + 1) if isinstance(tile, int) else ds(tile, 1)

            for hf in range(2):
                steps[0] += 1
                onehots(one(0), hf, steps[0])
            dve.wait_ge(S_ready, 2 * CHUNKS + 2)
            dve.wait_ge(h1_ready, TILES)
            dve.wait_ge(h0s_ready, TILES + 2)
            base = steps[0]
            with dve.Fori(0, 2) as half:
                for q in range(MK):
                    n = half * MK + q
                    dve.wait_ge(gate_ready, n + 1)
                    dve.wait_ge(gates_done, n * 2 + 2)
                    dve.scalar_tensor_tensor(mT[:, q, ds(half * HALF, HALF)], gate_out, WSCALE, bank[1][:, :],
                                             ALU.mult, ALU.mult).then_inc(hidden_free, 1)
                    tile = half * 2 + q // 2
                    multiply(one(tile), q % 2, n)
                    onehots(one(tile + 1), q % 2, half * MK + (base + q + 1))
            steps[0] += 2 * MK
            base = steps[0]
            with dve.Fori(0, TILES // 2 - 1) as i:
                for q in range(2):
                    tile = i + TILES // 2
                    multiply(one(tile), q, tile * 2 + q)
                    onehots(one(tile + 1), q, i * 2 + (base + q + 1))
            steps[0] += 2 * (TILES // 2 - 1)
            for q in range(2):
                multiply(one(TILES - 1), q, 2 * (TILES - 1) + q)

            def low_parts(first, end):
                with dve.Fori(first, end) as i:
                    for j in range(4):
                        dve.wait_ge(G_hi_ready, i * 4 + (j + 1))
                        dve.tensor_tensor(G_lo[:, j, :], S[:, ds(i * 4 + j, 1), HALF:2 * HALF]
                                          .rearrange("p c t -> p (c t)"), G_hi[:, j, :].bitcast(F32),
                                          ALU.subtract).then_inc(G_lo_ready, 1)

            for t in range(TILES):
                u = t % 2
                if t < TILES // 2:
                    low_parts(2 * t, 2 * t + 2)
                y2 = result[:, t % 4, :]
                dve.wait_ge(out_turned, t + 1)
                if t >= 4:
                    dve.wait_ge(stored[t % 4], 16)
                step(dve.tensor_tensor(y2, out_slot(t), h1[:, t, :], ALU.add))
                step(dve.bn_stats(stat(u, STATS, 6), y2))
                step(dve.bn_aggr(stat(u, MEAN, 2), stat(u, STATS, 6)))
                dve.tensor_scalar(stat(u, VAR_EPS), stat(u, VAR), EPS, None, ALU.add).then_inc(var2_ready, 1)
                dve.wait_ge(rstd2_ready, t + 1)
                dve.tensor_scalar(y2, y2, stat(u, MEAN), stat(u, RSTD),
                                  ALU.subtract, ALU.mult).then_inc(result_ready, 1)


_ARGS = ["x", "L0_tok_W", "L0_tok_b", "L0_tok_pos_emb", "L0_attn_W", "L0_ffn_w_queries", "L0_ffn_keys",
         "L0_ffn_down_embed", "L0_ffn_up_embed", "L0_ffn_w_gate", "L0_ffn_w_up", "L0_ffn_w_down"]


def constant_tables():
    import numpy as np

    row = np.arange(P)
    image, patch = row // PATCHES, row % PATCHES
    seen = (image[:, None] == image[None, :]) & (patch[None, :] <= patch[:, None])
    quadrant = row // 32
    return np.concatenate([np.eye(P), np.where(seen, 0.0, -3e38),
                           quadrant[:, None] % 2 == np.arange(2)[None, :]], axis=1).astype(np.float32)


def kernel(**inputs):
    import numpy as np
    import concourse.bacc as bacc
    from concourse.bass_utils import run_bass_kernel_spmd

    nc = bacc.Bacc("TRN2", target_bir_lowering=False, num_devices=1)
    arrays, args = {}, []
    named = [(name, np.ascontiguousarray(inputs[name])) for name in _ARGS] + [("constants", constant_tables())]
    for name, a in named:
        arrays[f"in_{name}"] = a
        args.append(nc.dram_tensor(f"in_{name}", a.shape, mybir.dt.from_np(a.dtype), kind="ExternalInput").ap())
    out = nc.dram_tensor("out_h", (IMAGES, PATCHES, D), F32, kind="ExternalOutput").ap()
    vit_block_kernel(nc, *args, out)
    run = run_bass_kernel_spmd(nc, [arrays], core_ids=[0])
    return run.results[0]["out_h"]
```

```python
from contextlib import ExitStack

import concourse.bass as bass
from concourse import mybir

P = 128
IMAGES, CHANNELS, SIDE, PATCH = 64, 3, 64, 16
GRID = SIDE // PATCH
PATCHES = GRID * GRID
D = 256
DK = D // P
TOKENS = IMAGES * PATCHES
TILES = TOKENS // P
FEATURES = CHANNELS * PATCH * PATCH
FK = FEATURES // P
HALF = TOKENS // 2
QUARTER = TOKENS // 4
HEADS, TOPK, KEYS = 4, 8, 128
PICKS = HEADS * TOPK
RET = 32
EXPERTS = 4096
CHUNKS = EXPERTS // P
INTER = 512
MK = INTER // P
EPS = 1e-5
WSCALE = float(2 ** 14)
STEP = 16
HALF_TILES = 2 * TILES
OVERLAPPED = HALF_TILES // 2 - 2

ALU = mybir.AluOpType
ACT = mybir.ActivationFunctionType
AX_X = mybir.AxisListType.X
F32 = mybir.dt.float32
F16 = mybir.dt.float16
F32R = mybir.dt.float32r
U32 = mybir.dt.uint32
ds = bass.ds


def vit_block_kernel(nc, x, tok_w, tok_b, pos_emb, attn_w, w_queries, keys, down_embed, up_embed,
                     w_gate, w_up, w_down, constants, out):
    with ExitStack() as ctx:
        def sb(name, shape, dt):
            return ctx.enter_context(nc.sbuf_tensor(name, shape, dt))

        def sem(name):
            return ctx.enter_context(nc.semaphore(name))

        def shared(*sets):
            handles = []
            for tensors in sets[:-1]:
                with ExitStack() as phase:
                    handles.append([phase.enter_context(nc.sbuf_tensor(*t)) for t in tensors])
            handles.append([sb(*t) for t in sets[-1]])
            return handles

        (early_inputs, xT_hi, xT_lo, tokwT_hi, tokwT_lo), (S,) = shared(
            [("early_inputs", [P, CHUNKS * TOKENS - 2 * FK * (HALF + D)], F32),
             ("xT_hi", [P, FK, HALF], F32R), ("xT_lo", [P, FK, HALF], F32R),
             ("tokwT_hi", [P, FK, D], F32R), ("tokwT_lo", [P, FK, D], F32R)],
            [("S", [P, CHUNKS, TOKENS], F32)])
        at = [0]

        def early(cols):
            at[0] += cols
            return early_inputs[:, at[0] - cols:at[0]]

        x_rows_flat = early(CHANNELS * 2 * PATCH * SIDE)
        x_rows = x_rows_flat.rearrange("p (c l m) -> p c l m", c=CHANNELS, l=2)
        x_feats = early(CHANNELS * 2 * PATCH * SIDE).rearrange("p (c l w f) -> p c l w f", c=CHANNELS, l=2, w=GRID)
        tokw_nat = early(DK * FEATURES).rearrange("p (o f) -> p o f", o=DK)
        attnw_nat = early(2 * DK * D).rearrange("p (o f) -> p o f", f=D)
        queryw_nat = early(DK * D).rearrange("p (o f) -> p o f", f=D)
        gatew_nat = early(MK * D).rearrange("p (o f) -> p o f", f=D)
        upw_nat = early(MK * D).rearrange("p (o f) -> p o f", f=D)
        downw_nat = early(DK * INTER).rearrange("p (o f) -> p o f", f=INTER)
        keys_nat = early(2 * P).rearrange("p (s f) -> p s f", f=P)
        pos_nat = early(D)
        attnwT = early(DK * 2 * D).rearrange("p (k o) -> p k o", o=2 * D)
        h0T = early(DK * TOKENS).rearrange("p (k t) -> p k t", t=TOKENS)
        posT = early(DK * PATCHES).rearrange("p (k n) -> p k n", n=PATCHES)
        bias_rows = early(D)
        mask = early(P)
        at_x = [0]

        def four(cols):
            at_x[0] += 4 * cols
            return x_rows_flat[:, at_x[0] - 4 * cols:at_x[0]].rearrange("p (u f) -> p u f", u=4)

        kv = four(2 * D)
        h0x2 = four(D)
        masked = four(P)
        probs = four(P)
        probsT = four(P)
        y1 = four(D)

        downwT = sb("downwT", [P, MK, D], F32)
        h1T = sb("h1T", [P, DK, TOKENS], F32)
        h1 = sb("h1", [P, TILES, D], F32)
        grid = sb("grid", [P, KEYS, STEP], F16)
        ident = sb("ident", [P, P], F32)
        slot_mask = sb("slot_mask", [P, 2], F32)
        iota8 = sb("iota8", [P, TOPK], F32)
        minus_half = sb("minus_half", [P, 1], F32)
        tab = sb("tab", [P, 4, D], F32)
        dT = sb("dT", [P, 2, DK, P], F32)
        selT = sb("selT", [P, TILES, 4, 32], F16)
        selW = sb("selW", [P, TILES, 2, 2, 32], F16)
        held = sb("held", [P, 2], F32)
        small = sb("small", [P, 64], F32)
        edge = sb("edge", [P, PICKS], F32)

        (h1T_hi, h1T_lo), (G_hi, G_lo), (mT,) = shared(
            [("h1T_hi", [P, DK, TOKENS], F32R), ("h1T_lo", [P, DK, TOKENS], F32R)],
            [("G_hi", [P, 4, HALF], F32R), ("G_lo", [P, 4, HALF], F32R)],
            [("mT", [P, MK, TOKENS], F32)])
        (up_hi, up_lo), (gatewT, upwT) = shared(
            [("up_hi", [P, 4, D], F32R), ("up_lo", [P, 4, D], F32R)],
            [("gatewT", [P, DK, INTER], F32), ("upwT", [P, DK, INTER], F32)])
        (keysB_t, querywT_t, qs_t, match_t, pair_sum_t, diffs_t, top_idx, pair_val, pair_pos, pair_ij, row_xy, dT_hi,
         dT_lo), (onehot_y, weighted_x) = shared(
                [("keysB", [P, 2, HEADS * KEYS], F32), ("querywT", [P, DK, D], F32), ("qs", [P, 2, P], F32),
                 ("match", [P, 2 * PICKS, TOPK], F32), ("pair_sum", [P, HEADS * TOPK * TOPK], F32),
                 ("diffs", [P, TILES, PICKS], F32),
                 ("top_idx", [P, 2, HEADS, TOPK], U32), ("pair_val", [P, HEADS, TOPK], F32),
                 ("pair_pos", [P, PICKS], U32), ("pair_ij", [P, 2, PICKS], U32), ("row_xy", [P, 2, PICKS], F32),
                 ("dT_hi", [P, 2, DK, P], F32R), ("dT_lo", [P, 2, DK, P], F32R)],
                [("onehot_y", [P, 2, KEYS, STEP], F16), ("weighted_x", [P, 2, 4, 32, STEP], F16)])
        keysB, querywT, qs = keysB_t[:, :, :], querywT_t[:, :, :], qs_t[:, :, :]
        querywT_flat = querywT.rearrange("p k o -> p (k o)")
        match, pair_sum, diffs = match_t[:, :, :], pair_sum_t[:, :], diffs_t[:, :, :]
        exps = match.rearrange("p a i -> p (a i)")[:, 0:TILES * PICKS].rearrange("p (t a) -> p t a", a=PICKS)
        onehot_x = sb("onehot_x", [P, 2, 32, STEP], F16)
        pack = onehot_x[:, :, :, :].rearrange("p u x s -> p (u x s)").rearrange(
            "p (t q a) -> p t q a", q=4, a=PICKS)

        top_val = sb("top_val", [P, 2, HEADS, TOPK], F32)

        late = h1T[:, :, :].rearrange("p k t -> p (k t)")
        outT = late[:, 0:1024].rearrange("p (k t) -> p k t", k=DK)
        result = late[:, 1024:2048].rearrange("p (r f) -> p r f", r=4)

        bank = [ctx.enter_context(nc.psum_tensor(f"bank{i}", [P, 512], F32)) for i in range(4)]
        region = [ctx.enter_context(nc.psum_tensor(f"region{i}", [P, 1024], F32)) for i in range(2)]
        turn = [region[0][:, 0:512], region[0][:, 512:1024], region[1][:, 0:512], region[1][:, 512:1024]]

        in_ident = sem("in_ident")
        in_const = sem("in_const")
        in_tokw = sem("in_tokw")
        in_x = [[sem(f"in_x{l}{c}") for c in range(CHANNELS)] for l in range(2)]
        sorted_by_dve = sem("sorted_by_dve")
        sorted_by_act = sem("sorted_by_act")
        in_attnw = sem("in_attnw")
        in_rest = sem("in_rest")
        in_tab = [sem(f"in_tab{j}") for j in range(4)]
        pool_ready = sem("pool_ready")
        turned = sem("turned")
        turned_by_act = sem("turned_by_act")
        turned_by_dve = sem("turned_by_dve")
        pos_biased = sem("pos_biased")
        pos_turned = sem("pos_turned")
        posT_ready = sem("posT_ready")
        keys_turned = sem("keys_turned")
        keysB_ready = sem("keysB_ready")
        embedded = sem("embedded")
        h0T_ready = sem("h0T_ready")
        keyT_done = sem("keyT_done")
        v_done = sem("v_done")
        keyT_ready = sem("keyT_ready")
        v_ready = sem("v_ready")
        scored = sem("scored")
        max_ready = sem("max_ready")
        probs_ready = sem("probs_ready")
        probs_turned = sem("probs_turned")
        probsT_ready = sem("probsT_ready")
        attended = sem("attended")
        var_ready = sem("var_ready")
        rstd_ready = sem("rstd_ready")
        h1_ready = sem("h1_ready")
        h1_turned = sem("h1_turned")
        query_done = sem("query_done")
        qs_ready = sem("qs_ready")
        sim_done = sem("sim_done")
        sims_read = sem("sims_read")
        tab_turned = sem("tab_turned")
        dT_hi_ready = sem("dT_hi_ready")
        dT_lo_ready = sem("dT_lo_ready")
        h1T_hi_ready = sem("h1T_hi_ready")
        h1T_lo_ready = sem("h1T_lo_ready")
        up_hi_ready = sem("up_hi_ready")
        up_lo_ready = sem("up_lo_ready")
        G_hi_ready = sem("G_hi_ready")
        G_lo_ready = sem("G_lo_ready")
        G_free = sem("G_free")
        dots_done = sem("dots_done")
        S_ready = sem("S_ready")
        diffs_ready = sem("diffs_ready")
        exps_ready = sem("exps_ready")
        gates_done = sem("gates_done")
        gate_out_done = sem("gate_out_done")
        hidden_out = sem("hidden_out")
        hidden_ready = sem("hidden_ready")
        onehots_ready = sem("onehots_ready")
        region_done = sem("region_done")
        region_free = sem("region_free")
        summed = sem("summed")
        outT_ready = sem("outT_ready")
        outT_by_dve = sem("outT_by_dve")
        out_turned = sem("out_turned")
        var2_ready = sem("var2_ready")
        rstd2_ready = sem("rstd2_ready")
        result_ready = sem("result_ready")
        stored = [sem(f"stored{r}") for r in range(4)]
        dve_step = sem("dve_step")

        block = ctx.enter_context(nc.Block())

        MEAN, VAR, VAR_EPS, RSTD, NEG_MAX, SUM, RECIP, STATS = range(8)

        def stat(u, n, cols=1):
            return small[:, 16 * u + n:16 * u + n + cols]

        def stats_of(tiles, n):
            u = tiles[0] % 4
            return small[:, :].rearrange("p (u c) -> p u c", c=16)[:, u:u + len(tiles), n]

        LATE_TILES = [(t,) for t in range(TILES // 2)] + [(t, t + 1) for t in range(TILES // 2, TILES, 2)]

        def blocks_of(nat, rows, k):
            return [nat[:, o, k * P:(k + 1) * P] for o in range(rows)]

        def x_blocks(l, k):
            c, i = divmod(k, 2)
            return [x_feats[:, c, l, w, i * P:(i + 1) * P] for w in range(GRID)]

        def two(dst, k):
            return dst[:, k:k + 2, :].rearrange("p k o -> p (k o)")

        in_rest_all = 7 * 16
        groups = [("tokw", [b for k in (g, g + 1) for b in blocks_of(tokw_nat, DK, k)],
                   (two(tokwT_hi, g), two(tokwT_lo, g)), in_tokw, 16)
                  for g in range(0, FK, 2)]
        groups += [(f"x{l}", x_blocks(l, k), (xT_hi[:, k, :], xT_lo[:, k, :]),
                    sorted_by_act if (CHANNELS * l + k // 2) % 2 else sorted_by_dve, (CHANNELS * l + k // 2) // 2 + 1)
                   for l in range(2) for k in range(FK)]
        groups += [("attnw", blocks_of(attnw_nat, 2 * DK, k), attnwT[:, k, :], in_attnw, 16) for k in range(DK)]
        groups += [("queryw", [b for k in range(DK) for b in blocks_of(queryw_nat, DK, k)], querywT_flat,
                    in_rest, in_rest_all)]
        groups += [("gatew", blocks_of(gatew_nat, MK, k), gatewT[:, k, :], in_rest, in_rest_all) for k in range(DK)]
        groups += [("upw", blocks_of(upw_nat, MK, k), upwT[:, k, :], in_rest, in_rest_all) for k in range(DK)]
        groups += [("downw", [b for k in (g, g + 1) for b in blocks_of(downw_nat, DK, k)], two(downwT, g),
                    in_rest, in_rest_all) for g in range(0, MK, 2)]
        names = [g[0] for g in groups]
        n_groups = len(groups)
        x0_starts, weights_start, late_start = names.index("x0"), names.index("attnw"), names.index("gatew") + 1

        act_sorts, dve_sorts = {2: 1, 5: 3, 9: 5}, {1: 0, 4: 2, 8: 4}

        def sort_x(engine, unit, done):
            l, c = divmod(unit, CHANNELS)
            engine.wait_ge(in_x[l][c], 32)
            src = x_rows[:, c, l, :].rearrange("p (i w j) -> p w i j", w=GRID, j=PATCH)
            dst = x_feats[:, c, l, :, :].rearrange("p w (i j) -> p w i j", j=PATCH)
            (engine.copy if done is sorted_by_act else engine.tensor_copy)(dst, src).then_inc(done, 1)

        def act_groups(g):
            return len([h for h in range(g) if h < weights_start or h % 2 == 0])

        def dve_groups(g):
            return len([h for h in range(g) if h < weights_start or h % 2 == 1])

        late_turn = [turn[0], turn[1], bank[1][:, :], bank[0][:, :], turn[3]]

        def turn_of(g):
            return turn[g % 4] if g < late_start else late_turn[g - late_start]

        sums = [[bank[2][:, :], bank[3][:, :]], [bank[0][:, :], bank[1][:, :]]]
        gate_out = dT[:, :, :, :].rearrange("p u k t -> p (u k t)")
        key_bank, v_bank, sum_bank = turn[2:4], bank[0:2], bank[2:4]
        down_rows = down_embed.rearrange("(c p) d -> p c d", p=P)
        up_rows = up_embed.rearrange("(c p) d -> p c d", p=P)

        def out_slot(t):
            return [bank[2][:, 0:D], bank[3][:, 0:D], region[0][:, 0:D], region[0][:, 512:512 + D]][t % 4]

        @block.sync
        def _(sp):
            sp.dma_start(ident[:, :], constants[:, 0:P]).then_inc(in_ident, 16)
            sp.dma_start(tokw_nat, tok_w.rearrange("(o p) f -> p o f", p=P)).then_inc(in_tokw, 16)
            image_rows = x.rearrange("b c (q l i) w -> q l b c i w", q=2, l=2, i=PATCH)
            for l in range(2):
                for c in range(CHANNELS):
                    for q in range(2):
                        sp.dma_start(x_rows[64 * q:64 * q + 64, c, l, :].rearrange("p (i w) -> p i w", w=SIDE),
                                     image_rows[q, l, :, c, :, :]).then_inc(in_x[l][c], 16)
                    if (l, c) == (0, 0):
                        sp.dma_start(pos_nat[0:PATCHES, :], pos_emb).then_inc(in_const, 16)
                        sp.dma_start(bias_rows[0:PATCHES, :], tok_b.partition_broadcast(PATCHES)).then_inc(in_const, 16)
                        sp.dma_start(slot_mask[:, :], constants[:, 2 * P:2 * P + 2]).then_inc(in_const, 16)
            sp.dma_start(attnw_nat, attn_w.rearrange("(o p) f -> p o f", p=P)).then_inc(in_attnw, 16)
            sp.dma_start(queryw_nat, w_queries.rearrange("(o p) f -> p o f", p=P)).then_inc(in_rest, 16)
            sp.dma_start(gatew_nat, w_gate.rearrange("(o p) f -> p o f", p=P)).then_inc(in_rest, 16)
            sp.dma_start(upw_nat, w_up.rearrange("(o p) f -> p o f", p=P)).then_inc(in_rest, 16)
            sp.dma_start(downw_nat, w_down.rearrange("(o p) f -> p o f", p=P)).then_inc(in_rest, 16)
            for s in range(2):
                sp.dma_start(keys_nat[:, s, :].rearrange("p (h n) -> p h n", h=HEADS),
                             keys.rearrange("h k s n -> s k h n")[s]).then_inc(in_rest, 16)
            sp.dma_start(mask, constants[:, P:2 * P]).then_inc(in_rest, 16)
            for j in range(4):
                sp.dma_start(tab[:, j, :], down_rows[:, j, :]).then_inc(in_tab[j], 16)
            with sp.Fori(1, TILES) as i:
                for j in range(4):
                    sp.wait_ge(tab_turned, i * 4 + (j - 3))
                    sp.dma_start(tab[:, j, :], down_rows[:, ds(i * 4 + j, 1), :].rearrange("p c d -> p (c d)")
                                 ).then_inc(in_tab[j], 16)
            for half in range(2):
                for j in range(4):
                    if half == 0:
                        sp.wait_ge(tab_turned, CHUNKS - 3 + j)
                    else:
                        sp.wait_ge(up_lo_ready, CHUNKS - 3 + j)
                    sp.dma_start(tab[:, j, :], up_rows[:, j, :]).then_inc(in_tab[j], 16)
                with sp.Fori(1, TILES) as i:
                    for j in range(4):
                        sp.wait_ge(up_lo_ready, i * 4 + (half * CHUNKS + j - 3))
                        sp.dma_start(tab[:, j, :], up_rows[:, ds(i * 4 + j, 1), :].rearrange("p c d -> p (c d)")
                                     ).then_inc(in_tab[j], 16)
            out_rows = out.rearrange("b n d -> (b n) d")
            for t in range(TILES):
                sp.wait_ge(result_ready, t + 1)
                sp.dma_start(out_rows[t * P:(t + 1) * P, :], result[:, t % 4, :]).then_inc(stored[t % 4], 16)
            for r in range(4):
                sp.wait_ge(stored[r], 16 * TILES // 4)

        @block.gpsimd
        def _(pool):
            pool.memset(keysB, 0.0).then_inc(pool_ready, 1)
            pool.memset(minus_half[:, :], -0.5).then_inc(pool_ready, 1)
            pool.iota(iota8[:, :], [[1, TOPK]], base=0, channel_multiplier=0,
                      allow_small_or_imprecise_dtypes=True).then_inc(pool_ready, 1)
            pool.iota(grid[:, :, :], [[1, KEYS], [0, STEP]], base=0, channel_multiplier=0,
                      allow_small_or_imprecise_dtypes=True).then_inc(pool_ready, 1)

            def split_dT(i, j):
                pool.wait_ge(dT_hi_ready, i * 4 + (j + 1))
                pool.tensor_tensor(dT_lo[:, j % 2, :, :], dT[:, j % 2, :, :], dT_hi[:, j % 2, :, :].bitcast(F32),
                                   ALU.subtract).then_inc(dT_lo_ready, 1)

            pool.wait_ge(pool_ready, 4)
            for k in range(TILES + 3):
                if 0 <= k - 2 < TILES:
                    pool.wait_ge(var_ready, k - 1)
                    pool.tensor_tensor(stat((k - 2) % 4, RSTD), stat((k - 2) % 4, VAR_EPS), minus_half[:, :],
                                       ALU.pow).then_inc(rstd_ready, 1)
                if k == TILES + 2:
                    split_dT(0, 0)
                if 0 <= k - 3:
                    cols = slice((k - 3) * P, (k - 2) * P)
                    pool.wait_ge(h1T_hi_ready, k - 2)
                    pool.tensor_tensor(h1T_lo[:, :, cols], h1T[:, :, cols], h1T_hi[:, :, cols].bitcast(F32),
                                       ALU.subtract).then_inc(h1T_lo_ready, 1)
            for j in range(1, 4):
                split_dT(0, j)
            with pool.Fori(1, TILES) as i:
                for j in range(4):
                    split_dT(i, j)

            pool.sem_inc(hidden_ready, 1)

            def hidden_block(half, q, n):
                block_m = mT[:, q, ds(half * HALF, HALF)]
                pool.wait_ge(hidden_out, n + 2)
                pool.tensor_tensor(block_m, block_m, gate_out, ALU.mult).then_inc(hidden_ready, 1)

            for half in range(2):
                hidden_block(half, 0, half)
            with pool.Fori(0, 2) as half:
                for q in range(1, MK):
                    hidden_block(half, q, half * (MK - 1) + (q + 1))

            def split_up(first, end):
                with pool.Fori(first, end) as i:
                    for j in range(4):
                        pool.wait_ge(up_hi_ready, i * 4 + (j + 1))
                        pool.tensor_tensor(up_lo[:, j, :], tab[:, j, :], up_hi[:, j, :].bitcast(F32),
                                           ALU.subtract).then_inc(up_lo_ready, 1)

            split_up(0, TILES)
            for tiles in LATE_TILES:
                if tiles[0] < TILES // 2:
                    split_up(TILES + 2 * tiles[0], TILES + 2 * tiles[0] + 2)
                pool.wait_ge(var2_ready, tiles[-1] + 1)
                pool.tensor_tensor(stats_of(tiles, RSTD), stats_of(tiles, VAR_EPS),
                                   minus_half[:, :].broadcast_to([P, len(tiles)]),
                                   ALU.pow).then_inc(rstd2_ready, len(tiles))

        @block.tensor
        def _(pe):
            def turn_group(g):
                _, blocks, _, arrived, value = groups[g]
                pe.wait_ge(arrived, value)
                if g >= late_start:
                    pe.wait_ge(keysB_ready, HEADS)
                    if g >= late_start + 2:
                        pe.wait_ge(v_ready, TILES)
                elif g >= 4:
                    if g - 4 < weights_start or g % 2 == 1:
                        pe.wait_ge(turned_by_dve, dve_groups(g - 3))
                    else:
                        pe.wait_ge(turned_by_act, act_groups(g - 3))
                for n, b in enumerate(blocks):
                    last = pe.transpose(turn_of(g)[:, n * P:(n + 1) * P], b, ident[:, :])
                last.then_inc(turned, 1)

            def channel_groups(m):
                return range(x0_starts + 2 * m, x0_starts + 2 * m + 2)

            def embed(m):
                l, c = divmod(m, CHANNELS)
                taken = channel_groups(m)[-1] + 1
                pe.wait_ge(turned_by_dve, taken)
                for o in range(DK):
                    for k in (2 * c, 2 * c + 1):
                        for n, (a, b) in enumerate(((tokwT_hi, xT_hi), (tokwT_hi, xT_lo), (tokwT_lo, xT_hi))):
                            last = pe.matmul(bank[2 * l + o][:, :], a[:, k, o * P:(o + 1) * P], b[:, k, :],
                                             start=(k == 0 and n == 0), stop=(k == FK - 1 and n == 2))
                    if c == CHANNELS - 1:
                        last.then_inc(embedded, 1)

            pe.wait_ge(in_ident, 16)
            for g in range(x0_starts):
                turn_group(g)
            for m in range(2 * CHANNELS):
                if m == CHANNELS:
                    pe.wait_ge(posT_ready, 1)
                for g in channel_groups(m):
                    turn_group(g)
                if m == 2:
                    pe.wait_ge(pos_biased, 1)
                    for k in range(DK):
                        last = pe.transpose(bank[3][:, k * PATCHES:(k + 1) * PATCHES],
                                            pos_nat[0:PATCHES, k * P:(k + 1) * P], ident[0:PATCHES, 0:PATCHES])
                    last.then_inc(pos_turned, 1)
                if m > 0:
                    embed(m - 1)
            for g in range(weights_start, late_start):
                turn_group(g)
            embed(2 * CHANNELS - 1)
            pe.wait_ge(turned_by_act, act_groups(late_start))
            pe.wait_ge(turned_by_dve, dve_groups(late_start))
            for s in range(2):
                last = pe.transpose(turn[0][:, s * P:(s + 1) * P], keys_nat[:, s, :], ident[:, :])
            last.then_inc(keys_turned, 1)

            def turn_chunk(i, j):
                pe.wait_ge(in_tab[j], i * 16 + 16)
                for k in range(DK):
                    last = pe.transpose(bank[j % 2][:, k * P:(k + 1) * P],
                                        tab[:, j, k * P:(k + 1) * P], ident[:, :])
                last.then_inc(tab_turned, 1)

            def query(i):
                for s in range(2):
                    for k in range(DK):
                        last = pe.matmul(region[1][:, s * P:(s + 1) * P], querywT[:, k, s * P:(s + 1) * P],
                                         h1T[:, k, ds(i * P, P)], start=(k == 0), stop=(k == DK - 1))
                last.then_inc(query_done, 1)

            def similarities(i):
                pe.wait_ge(qs_ready, i + 1)
                for s in range(2):
                    for g in range(2):
                        rows = slice(64 * g, 64 * g + 64)
                        last = pe.matmul(region[0][:, 512 * g + 256 * s:512 * g + 256 * (s + 1)], qs[rows, s, :],
                                         keysB[rows, s, 256 * g:256 * (g + 1)], start=True, stop=True)
                last.then_inc(sim_done, 1)

            pe.wait_ge(h0T_ready, 4)
            for k in range(TILES + 3):
                if 0 <= k - 1 < TILES:
                    t, u, b = k - 1, (k - 1) % 4, (k - 1) % 2
                    pe.wait_ge(keyT_ready, t + 1)
                    for o in range(DK):
                        last = pe.matmul(key_bank[b][:, D:D + P], h0T[:, o, t * P:(t + 1) * P],
                                         kv[:, u, o * P:(o + 1) * P], start=(o == 0), stop=(o == DK - 1))
                    last.then_inc(scored, 1)
                if k < TILES:
                    t, b = k, k % 2
                    if t >= 2:
                        pe.wait_ge(probsT_ready, t - 1)
                    for o in range(DK):
                        for f in range(DK):
                            last = pe.matmul(key_bank[b][:, o * P:(o + 1) * P], attnwT[:, f, o * P:(o + 1) * P],
                                             h0T[:, f, t * P:(t + 1) * P], start=(f == 0), stop=(f == DK - 1))
                    last.then_inc(keyT_done, 1)
                    if t >= 2:
                        pe.wait_ge(v_ready, t - 1)
                    for f in range(DK):
                        pe.matmul(v_bank[b][:, 0:D], h0T[:, f, t * P:(t + 1) * P], attnwT[:, f, D:2 * D],
                                  start=(f == 0), stop=(f == DK - 1))
                    for f in range(DK):
                        last = pe.transpose(v_bank[b][:, D + f * P:D + (f + 1) * P],
                                            h0T[:, f, t * P:(t + 1) * P], ident[:, :])
                    last.then_inc(v_done, 1)
                if k == TILES:
                    for g in range(late_start, n_groups - 1):
                        turn_group(g)
                if 0 <= k - 1 < TILES:
                    t, u, b = k - 1, (k - 1) % 4, (k - 1) % 2
                    pe.wait_ge(probs_ready, t + 1)
                    pe.transpose(key_bank[b][:, D + P:2 * D], probs[:, u, :], ident[:, :]).then_inc(probs_turned, 1)
                if 0 <= k - 2 < TILES:
                    t, u, b = k - 2, (k - 2) % 4, (k - 2) % 2
                    pe.wait_ge(probsT_ready, t + 1)
                    pe.wait_ge(v_ready, t + 1)
                    if t >= 2:
                        pe.wait_ge(h1T_hi_ready, t - 1)
                    pe.matmul(sum_bank[b][:, 0:D], probsT[:, u, :], kv[:, u, D:2 * D],
                              start=True, stop=True).then_inc(attended, 1)
                if k == TILES + 1:
                    turn_group(n_groups - 1)
                    query(0)
                if 0 <= k - 3:
                    t, b = k - 3, (k - 3) % 2
                    pe.wait_ge(h1_ready, t + 1)
                    for f in range(DK):
                        last = pe.transpose(sum_bank[b][:, D + f * P:D + (f + 1) * P],
                                            h1[:, t, f * P:(f + 1) * P], ident[:, :])
                    last.then_inc(h1_turned, 1)
                if k == TILES + 2:
                    pe.wait_ge(turned_by_dve, dve_groups(late_start + 1))
                    similarities(0)
                if k == TILES + 1:
                    pe.wait_ge(turned_by_act, act_groups(n_groups))
                    turn_chunk(0, 0)

            pe.wait_ge(turned_by_dve, dve_groups(n_groups))
            pe.wait_ge(h1T_lo_ready, TILES // 2)

            def dots(i, j):
                pe.wait_ge(dT_lo_ready, i * 4 + (j + 1))
                for half in range(2):
                    if half == 1 and j == 0:
                        pe.wait_ge(h1T_lo_ready, TILES)
                    pe.wait_ge(S_ready, i * 8 + (2 * j + half + 1))
                    parts = ((dT_hi, h1T_hi), (dT_hi, h1T_lo), (dT_lo, h1T_hi))
                    for k in range(DK):
                        for n, (a, b) in enumerate(parts):
                            last = pe.matmul(bank[2 + half][:, :], a[:, j % 2, k, :],
                                             b[:, k, half * HALF:(half + 1) * HALF],
                                             start=(k == 0 and n == 0), stop=(k == DK - 1 and n == 2))
                    last.then_inc(dots_done, 1)

            def look_up(i, is_last):
                turn_chunk(i, 1)
                dots(i, 0)
                turn_chunk(i, 2)
                dots(i, 1)
                if not is_last:
                    query(i + 1)
                turn_chunk(i, 3)
                dots(i, 2)
                if not is_last:
                    turn_chunk(i + 1, 0)
                    pe.wait_ge(sims_read, i + 1)
                    similarities(i + 1)
                dots(i, 3)

            with pe.Fori(0, TILES - 1) as i:
                look_up(i, False)
            look_up(TILES - 1, True)

            def build_C(n, parity):
                pe.wait_ge(onehots_ready, n + 1)
                pe.wait_ge(region_free, n * 2 + 2)
                for s in range(STEP):
                    for part in range(2):
                        for g in range(2):
                            last = pe.matmul(region[g][:, s * 64:(s + 1) * 64],
                                             onehot_y[64 * g:64 * g + 64, parity, :, s],
                                             weighted_x[64 * g:64 * g + 64, parity, 2 * part:2 * part + 2, :, s],
                                             start=(part == 0), stop=(part == 1))
                last.then_inc(region_done, 1)

            def hidden(half, q, n):
                for b, w, read in ((0, gatewT, gate_out_done), (1, upwT, hidden_out)):
                    pe.wait_ge(read, n + 1)
                    for k in range(DK):
                        last = pe.matmul(bank[b][:, :], w[:, k, q * P:(q + 1) * P],
                                         h1T[:, k, ds(half * HALF, HALF)], start=(k == 0), stop=(k == DK - 1))
                    last.then_inc(gates_done, 1)

            def add_mlp(half, blocks):
                for fk in blocks:
                    for o in range(DK):
                        last = pe.matmul(sums[half][o], downwT[:, fk, o * P:(o + 1) * P],
                                         mT[:, fk, half * HALF:(half + 1) * HALF],
                                         start=(fk == 0), stop=False, skip_group_check=True)
                return last

            for half in range(2):
                hidden(half, 0, half)
            pe.wait_ge(S_ready, 2 * CHUNKS + 2)
            pe.wait_ge(hidden_ready, 2)
            add_mlp(0, (0,))
            with pe.Fori(0, 2) as half:
                for q in range(MK):
                    build_C(half * MK + q, q % 2)
                    if q + 1 < MK:
                        hidden(half, q + 1, half * (MK - 1) + (q + 2))
                    else:
                        for fk in range(1, MK):
                            pe.wait_ge(hidden_ready, 1 + (fk + 2))
                            for o in range(DK):
                                pe.matmul(bank[2 + o][:, ds(half * QUARTER, QUARTER)],
                                          downwT[:, fk, o * P:(o + 1) * P], mT[:, fk, ds(half * QUARTER, QUARTER)],
                                          start=False, stop=False, skip_group_check=True)

            def add_chunks(half, i, is_last=False):
                order = [(o, j) for o in range(DK) for j in range(4)] if is_last else \
                    [(o, j) for j in range(4) for o in range(DK)]
                for o, j in order:
                    if o == 0:
                        pe.wait_ge(up_lo_ready, i * 4 + (j + 1))
                        pe.wait_ge(G_lo_ready, i * 4 + (j + 1))
                    for n, (a, b) in enumerate(((up_hi, G_hi), (up_hi, G_lo), (up_lo, G_hi))):
                        last = pe.matmul(sums[half][o], a[:, j, o * P:(o + 1) * P], b[:, j, :], start=False,
                                         stop=(is_last and j == 3 and n == 2), skip_group_check=True)
                    if o == DK - 1:
                        last.then_inc(G_free, 1)
                    elif is_last and j == 3:
                        last.then_inc(summed, 1)

            def turn_output(half):
                pe.wait_ge(outT_ready, DK + half)
                if half:
                    pe.wait_ge(outT_by_dve, 1)
                    pe.wait_ge(var2_ready, TILES // 2)
                for t in range(TILES // 2 * half, TILES // 2 * (half + 1)):
                    a = t % (TILES // 2) * P
                    for o in range(DK):
                        last = pe.transpose(out_slot(t)[:, o * P:(o + 1) * P], outT[:, o, a:a + P], ident[:, :])
                    last.then_inc(out_turned, 1)

            pe.wait_ge(hidden_ready, 2 * MK + 1)
            pe.wait_ge(hidden_out, 2 * MK + 1)
            add_mlp(1, (0, 1))
            build_C(HALF_TILES // 2, 0)
            add_mlp(1, (2, 3)).then_inc(G_free, 4)
            build_C(HALF_TILES // 2 + 1, 1)
            with pe.Fori(0, OVERLAPPED // 2) as i:
                for q in range(2):
                    add_chunks(0, i * 2 + q)
                    build_C(i * 2 + (HALF_TILES // 2 + 2 + q), q)
            with pe.Fori(OVERLAPPED, TILES - 1) as i:
                add_chunks(0, i)
            add_chunks(0, TILES - 1, is_last=True)
            pe.wait_ge(region_free, 2 * HALF_TILES + 2)
            add_chunks(1, TILES)
            turn_output(0)
            with pe.Fori(TILES + 1, 2 * TILES - 1) as i:
                add_chunks(1, i)
            add_chunks(1, 2 * TILES - 1, is_last=True)
            turn_output(1)

        @block.scalar
        def _(act):
            def take_out(first, end):
                for g in range(first, end):
                    if g in act_sorts:
                        sort_x(act, act_sorts[g], sorted_by_act)
                    if g < weights_start:
                        act.wait_ge(turned, g + 1)
                        act.copy(groups[g][2][0], turn_of(g)).then_inc(turned_by_act, 1)
                    elif g % 2 == 0:
                        act.wait_ge(turned, g + 1)
                        act.copy(groups[g][2], turn_of(g)).then_inc(turned_by_act, 1)

            take_out(0, late_start)
            act.wait_ge(keys_turned, 1)
            act.wait_ge(pool_ready, 1)
            for h in range(HEADS):
                act.copy(keysB[RET * h:RET * (h + 1), :, h * KEYS:(h + 1) * KEYS],
                         turn[0][RET * h:RET * (h + 1), 0:256].rearrange("p (s k) -> p s k", s=2)
                         ).then_inc(keysB_ready, 1)

            def chunk_out(i, j):
                act.wait_ge(tab_turned, i * 4 + (j + 1))
                turned_chunk = bank[j % 2][:, 0:256].rearrange("p (k t) -> p k t", k=DK)
                act.copy(dT[:, j % 2, :, :], turned_chunk)
                act.copy(dT_hi[:, j % 2, :, :], turned_chunk).then_inc(dT_hi_ready, 1)

            def query_out(i):
                act.wait_ge(query_done, i + 1)
                act.copy(qs, region[1][:, 0:256].rearrange("p (s t) -> p s t", s=2)).then_inc(qs_ready, 1)

            for k in range(TILES + 3):
                if k == TILES + 2:
                    act.sem_inc(S_ready, 2)
                    act.activation(held[:, 1:2], minus_half[:, :], ACT.Silu)
                    chunk_out(0, 0)
                if 0 <= k - 1 < TILES:
                    t, u = k - 1, (k - 1) % 4
                    act.wait_ge(max_ready, t + 1)
                    act.activation(probs[:, u, :], masked[:, u, :], ACT.Exp, bias=stat(u, NEG_MAX),
                                   accum_out=stat(u, SUM)).then_inc(probs_ready, 1)
                if k < TILES:
                    t, u, b = k, k % 4, k % 2
                    act.wait_ge(keyT_done, t + 1)
                    act.copy(kv[:, u, 0:D], key_bank[b][:, 0:D]).then_inc(keyT_ready, 1)
                    act.wait_ge(v_done, t + 1)
                    act.copy(kv[:, u, D:2 * D], v_bank[b][:, 0:D])
                    act.mul(h0x2[:, u, :], v_bank[b][:, D:2 * D], 2.0).then_inc(v_ready, 1)
                if 0 <= k - 1 < TILES:
                    t, u, b = k - 1, (k - 1) % 4, (k - 1) % 2
                    act.wait_ge(probs_turned, t + 1)
                    act.copy(probsT[:, u, :], key_bank[b][:, D + P:2 * D]).then_inc(probsT_ready, 1)
                if k == TILES + 1:
                    query_out(0)
                if 0 <= k - 3:
                    t, b = k - 3, (k - 3) % 2
                    act.wait_ge(h1_turned, t + 1)
                    turned_h1 = sum_bank[b][:, D:2 * D].rearrange("p (k t) -> p k t", k=DK)
                    act.copy(h1T[:, :, t * P:(t + 1) * P], turned_h1)
                    act.copy(h1T_hi[:, :, t * P:(t + 1) * P], turned_h1).then_inc(h1T_hi_ready, 1)
                if k == TILES:
                    take_out(late_start, n_groups)

            def silu(i, j):
                for half in range(2):
                    act.wait_ge(dots_done, i * 8 + (2 * j + half + 1))
                    act.activation(S[:, ds(i * 4 + j, 1), half * HALF:(half + 1) * HALF]
                                   .rearrange("p c t -> p (c t)"), bank[2 + half][:, :], ACT.Silu
                                   ).then_inc(S_ready, 1)

            def look_up(i, is_last):
                chunk_out(i, 1)
                silu(i, 0)
                chunk_out(i, 2)
                silu(i, 1)
                if not is_last:
                    query_out(i + 1)
                chunk_out(i, 3)
                silu(i, 2)
                if is_last:
                    softmax_exps()
                else:
                    chunk_out(i + 1, 0)
                silu(i, 3)

            def softmax_exps():
                act.wait_ge(diffs_ready, TILES)
                act.activation(exps, diffs, ACT.Exp).then_inc(exps_ready, 1)

            with act.Fori(0, TILES - 1) as i:
                look_up(i, False)
            look_up(TILES - 1, True)

            act.sem_inc(hidden_out, 1)
            act.sem_inc(gate_out_done, 1)

            def hidden_block(half, q, n):
                act.wait_ge(gates_done, n * 2 + 1)
                act.wait_ge(hidden_ready, n + 1)
                act.activation(gate_out, bank[0][:, :], ACT.Silu).then_inc(gate_out_done, 1)
                act.wait_ge(gates_done, n * 2 + 2)
                act.mul(mT[:, q, ds(half * HALF, HALF)], bank[1][:, :], WSCALE).then_inc(hidden_out, 1)

            for half in range(2):
                hidden_block(half, 0, half)
            with act.Fori(0, 2) as half:
                for q in range(1, MK):
                    hidden_block(half, q, half * (MK - 1) + (q + 1))

            def split_chunks(half, first, end):
                with act.Fori(first, end) as i:
                    for j in range(4):
                        act.wait_ge(G_free, i * 4 + (j + 1))
                        act.wait_ge(in_tab[j], i * 16 + 16 * (TILES + 1))
                        act.copy(up_hi[:, j, :], tab[:, j, :]).then_inc(up_hi_ready, 1)
                        act.copy(G_hi[:, j, :], S[:, ds(i * 4 + (j - CHUNKS * half), 1), half * HALF:(half + 1) * HALF]
                                 .rearrange("p c t -> p (c t)")).then_inc(G_hi_ready, 1)

            def sums_out(half):
                for o in range(DK - half):
                    if o == 0:
                        act.wait_ge(summed, half + 1)
                    else:
                        act.wait_ge(G_free, 4 + CHUNKS * (half + 1))
                    act.mul(outT[:, o, :], sums[half][o], 1.0 / WSCALE).then_inc(outT_ready, 1)

            act.wait_ge(region_free, HALF_TILES + 2)
            split_chunks(0, 0, TILES)
            act.wait_ge(region_free, 2 * HALF_TILES + 2)
            split_chunks(1, TILES, TILES + 1)
            sums_out(0)
            split_chunks(1, TILES + 1, 2 * TILES)
            act.wait_ge(out_turned, TILES // 2)
            sums_out(1)

        @block.vector
        def _(dve):
            steps = [0]

            def step(ins):
                steps[0] += 1
                ins.then_inc(dve_step, 1)
                dve.wait_ge(dve_step, steps[0])

            def hold():
                dve.memset(held[:, 0:1], 0.0)

            def embed_out(l):
                for o in range(DK):
                    dve.wait_ge(embedded, 2 * l + o + 1)
                    dve.tensor_tensor(
                        h0T[:, o, :].rearrange("p (b q l w) -> p l w q b", q=2, l=2, w=GRID)[:, l],
                        bank[2 * l + o][:, :].rearrange("p (w q b) -> p w q b", w=GRID, q=2),
                        posT[:, o, :].rearrange("p (q l w) -> p l w q", q=2, l=2)[:, l].unsqueeze(3)
                        .broadcast_to([P, GRID, 2, IMAGES]), ALU.add).then_inc(h0T_ready, 1)

            def take_out(first, end):
                for g in range(first, end):
                    if g in dve_sorts:
                        sort_x(dve, dve_sorts[g], sorted_by_dve)
                    if g < weights_start:
                        high, low = groups[g][2]
                        dve.wait_ge(turned_by_act, g + 1)
                        dve.tensor_tensor(low, turn_of(g), high.bitcast(F32), ALU.subtract).then_inc(turned_by_dve, 1)
                    elif g % 2 == 1:
                        dve.wait_ge(turned, g + 1)
                        dve.tensor_copy(groups[g][2], turn_of(g)).then_inc(turned_by_dve, 1)

            first_half_turned = x0_starts + 2 * (CHANNELS + 1)
            take_out(0, x0_starts + 4)
            dve.wait_ge(in_const, 48)
            dve.tensor_tensor(pos_nat[0:PATCHES, :], pos_nat[0:PATCHES, :], bias_rows[0:PATCHES, :], ALU.add
                              ).then_inc(pos_biased, 1)
            dve.wait_ge(pos_turned, 1)
            dve.tensor_copy(posT, bank[3][:, 0:DK * PATCHES].rearrange("p (k n) -> p k n", k=DK)
                            ).then_inc(posT_ready, 1)
            dve.wait_ge(posT_ready, 1)
            take_out(x0_starts + 4, first_half_turned)
            embed_out(0)
            take_out(first_half_turned, late_start)
            embed_out(1)

            dve.sem_inc(region_free, 2)

            def to_h1(t):
                u = t % 4
                dve.wait_ge(rstd_ready, t + 1)
                dve.tensor_scalar(h1[:, t, :], y1[:, u, :], stat(u, MEAN), stat(u, RSTD),
                                  ALU.subtract, ALU.mult).then_inc(h1_ready, 1)

            dve.wait_ge(in_rest, in_rest_all)
            for k in range(TILES + 3):
                if 0 <= k - 1 < TILES:
                    t, u, b = k - 1, (k - 1) % 4, (k - 1) % 2
                    dve.wait_ge(scored, t + 1)
                    step(dve.tensor_tensor(masked[:, u, :], key_bank[b][:, D:D + P], mask, ALU.add))
                    dve.tensor_reduce(stat(u, NEG_MAX), masked[:, u, :], AX_X, ALU.max, negate=True
                                      ).then_inc(max_ready, 1)
                if 0 <= k - 3 and k != TILES + 1:
                    to_h1(k - 3)
                if 0 <= k - 2 < TILES:
                    t, u, b = k - 2, (k - 2) % 4, (k - 2) % 2
                    dve.wait_ge(probs_ready, t + 1)
                    dve.wait_ge(v_ready, t + 1)
                    step(dve.reciprocal(stat(u, RECIP), stat(u, SUM)))
                    dve.wait_ge(attended, t + 1)
                    step(dve.scalar_tensor_tensor(y1[:, u, :], sum_bank[b][:, 0:D], stat(u, RECIP),
                                                  h0x2[:, u, :], ALU.mult, ALU.add))
                if k == TILES + 1:
                    to_h1(k - 3)
                if 0 <= k - 2 < TILES:
                    t, u = k - 2, (k - 2) % 4
                    step(dve.bn_stats(stat(u, STATS, 6), y1[:, u, :]))
                    step(dve.bn_aggr(stat(u, MEAN, 2), stat(u, STATS, 6)))
                    dve.tensor_scalar(stat(u, VAR_EPS), stat(u, VAR), EPS, None, ALU.add).then_inc(var_ready, 1)
                if k == TILES + 1:
                    take_out(late_start, late_start + 1)
                if k == TILES + 2:
                    take_out(late_start + 1, n_groups)

            look_up_base = steps[0]
            per_tile = 10
            dve.wait_ge(pool_ready, 4)
            with dve.Fori(0, TILES) as i:
                n = [0]

                def chain(ins):
                    n[0] += 1
                    ins.then_inc(dve_step, 1)
                    dve.wait_ge(dve_step, i * per_tile + (look_up_base + n[0]))

                def sims(s, h):
                    g, h2 = divmod(h, 2)
                    first = 512 * g + 256 * s + KEYS * h2
                    return region[0][:, first:first + KEYS]

                pairs = [(s, h) for s in range(2) for h in range(HEADS)]
                dve.wait_ge(sim_done, i + 1)
                hold()
                for s, h in pairs:
                    last = dve.max(top_val[:, s, h, :], sims(s, h))
                chain(last)
                hold()
                for s, h in pairs:
                    last = dve.max_index(top_idx[:, s, h, :], top_val[:, s, h, :], sims(s, h))
                last.then_inc(sims_read, 1)
                chain(dve.tensor_tensor(
                    pair_sum.rearrange("p (h i j) -> p h i j", h=HEADS, i=TOPK),
                    top_val[:, 0].unsqueeze(3).broadcast_to([P, HEADS, TOPK, TOPK]),
                    top_val[:, 1].unsqueeze(2).broadcast_to([P, HEADS, TOPK, TOPK]), ALU.add))
                hold()
                for h in range(HEADS):
                    last = dve.max(pair_val[:, h, :], pair_sum[:, h * 64:(h + 1) * 64])
                chain(last)
                hold()
                for h in range(HEADS):
                    last = dve.max_index(pair_pos[:, h * TOPK:(h + 1) * TOPK], pair_val[:, h, :],
                                         pair_sum[:, h * 64:(h + 1) * 64])
                chain(last)
                dve.tensor_scalar(pair_ij[:, 0, :], pair_pos[:, :], 3, None, ALU.logical_shift_right)
                chain(dve.tensor_scalar(pair_ij[:, 1, :], pair_pos[:, :], TOPK - 1, None, ALU.bitwise_and))
                chain(dve.tensor_tensor(
                    match, pair_ij[:, :, :].rearrange("p s a -> p (s a)").unsqueeze(2)
                    .broadcast_to([P, 2 * PICKS, TOPK]),
                    iota8[:, :].unsqueeze(1).broadcast_to([P, 2 * PICKS, TOPK]), ALU.is_equal))
                dve.wait_ge(sims_read, i + 1)
                chain(dve.tensor_tensor(
                    match.rearrange("p (g k) i -> p g k i", k=TOPK),
                    match.rearrange("p (g k) i -> p g k i", k=TOPK),
                    top_idx[:, :, :, :].rearrange("p s h i -> p (s h) i").unsqueeze(2)
                    .broadcast_to([P, 2 * HEADS, TOPK, TOPK]), ALU.mult))
                chain(dve.tensor_reduce(row_xy[:, :, :].rearrange("p s a -> p (s a)"), match, AX_X, ALU.add))
                chain(dve.tensor_scalar(edge[:, :], row_xy[:, 0, :], float(CHUNKS), float(KEYS - 1),
                                        ALU.is_ge, ALU.mult))
                dve.tensor_scalar(pack[:, ds(i, 1), 0, :].rearrange("p t a -> p (t a)"), row_xy[:, 0, :],
                                  float(CHUNKS - 1), None, ALU.min)
                chain(dve.tensor_tensor(pack[:, ds(i, 1), 1, :].rearrange("p t a -> p (t a)"), row_xy[:, 1, :],
                                        edge[:, :], ALU.max))
                dve.tensor_tensor(diffs[:, ds(i, 1), :].rearrange("p t (h k) -> p (t h) k", h=HEADS), pair_val[:, :, :],
                                  pair_val[:, :, 0:1].broadcast_to([P, HEADS, TOPK]), ALU.subtract
                                  ).then_inc(diffs_ready, 1)
                assert n[0] == per_tile, n[0]
            steps[0] += per_tile * TILES

            step(dve.transpose(selT[:, :, 0:2, :].rearrange("p t q s -> p t (q s)"),
                               pack[:, :, 0:2, :].rearrange("p t q a -> p t (q a)")))

            heads = "p t (h k) -> p (t h) k"
            sums8 = top_val[:, :, :, :].rearrange("p s h k -> p (s h k)")[:, 0:32]
            recips = top_val[:, :, :, :].rearrange("p s h k -> p (s h k)")[:, 32:64]
            dve.wait_ge(exps_ready, 1)
            step(dve.tensor_reduce(sums8, exps.rearrange(heads, h=HEADS), AX_X, ALU.add))
            step(dve.reciprocal(recips, sums8))
            step(dve.scalar_tensor_tensor(diffs.rearrange(heads, h=HEADS), exps.rearrange(heads, h=HEADS), WSCALE,
                                          recips.unsqueeze(2).broadcast_to([P, TILES * HEADS, TOPK]),
                                          ALU.mult, ALU.mult))
            step(dve.tensor_copy(pack[:, :, 2, :], diffs))
            step(dve.tensor_tensor(pack[:, :, 3, :], diffs, pack[:, :, 2, :], ALU.subtract))
            step(dve.transpose(selT[:, :, 2:4, :].rearrange("p t q s -> p t (q s)"),
                               pack[:, :, 2:4, :].rearrange("p t q a -> p t (q a)")))
            for slot in range(2):
                last = dve.tensor_scalar(selW[:, :, :, slot, :], selT[:, :, 2:4, :], slot_mask[:, slot:slot + 1],
                                         None, ALU.mult)
            step(last)

            def onehots_xy(tile, hf):
                cols = slice(STEP * hf, STEP * (hf + 1))
                dve.tensor_tensor(onehot_x[:, hf, :, :], grid[:, 0:32, :],
                                  selT[:, tile, 0, cols].broadcast_to([P, 32, STEP]), ALU.is_equal
                                  ).then_inc(dve_step, 1)
                dve.tensor_tensor(onehot_y[:, hf, :, :], grid[:, :, :],
                                  selT[:, tile, 1, cols].broadcast_to([P, KEYS, STEP]), ALU.is_equal)

            def weigh_x(tile, hf, x_done):
                cols = slice(STEP * hf, STEP * (hf + 1))
                dve.wait_ge(dve_step, x_done)
                dve.tensor_tensor(weighted_x[:, hf, :, :, :],
                                  onehot_x[:, hf:hf + 1, :, :].broadcast_to([P, 4, 32, STEP]),
                                  selW[:, tile, :, :, cols].rearrange("p t a b s -> p (t a b) s").unsqueeze(2)
                                  .broadcast_to([P, 4, 32, STEP]), ALU.mult).then_inc(onehots_ready, 1)

            def onehots(tile, hf, x_done):
                onehots_xy(tile, hf)
                weigh_x(tile, hf, x_done)

            S_tiles = S[:, :, :].rearrange("p x (n b t) -> p x n b t", n=TILES, b=4)

            def multiply(tile, hf, n, regions=(0, 1)):
                for g in regions:
                    dve.wait_ge(region_done, n + 1)
                    block_S = S_tiles[:, :, tile, 2 * g:2 * g + 2, STEP * hf:STEP * (hf + 1)].rearrange(
                        "p x n b t -> p x (n b) t")
                    dve.tensor_tensor(block_S, region[g][:, :].rearrange("p (s b x) -> p x b s", s=STEP, b=2),
                                      block_S, ALU.mult).then_inc(region_free, 1)

            def one(tile):
                return slice(tile, tile + 1) if isinstance(tile, int) else ds(tile, 1)

            for hf in range(2):
                steps[0] += 1
                if hf:
                    dve.wait_ge(dots_done, 2 * CHUNKS)
                onehots(one(0), hf, steps[0])
            dve.wait_ge(S_ready, 2 * CHUNKS + 2)
            with dve.Fori(0, TILES // 2) as i:
                for q in range(2):
                    multiply(one(i), q, i * 2 + q)
                    onehots(one(i + 1), q, i * 2 + (steps[0] + q + 1))
            steps[0] += HALF_TILES // 2
            half_tile = HALF_TILES // 2
            multiply(one(TILES // 2), 0, half_tile)
            steps[0] += 1
            onehots(one(TILES // 2 + 1), 0, steps[0])

            def low_part(half, i, j):
                dve.wait_ge(G_hi_ready, i * 4 + (j + 1))
                dve.tensor_tensor(G_lo[:, j, :], S[:, ds(i * 4 + (j - CHUNKS * half), 1), half * HALF:(half + 1) * HALF]
                                  .rearrange("p c t -> p (c t)"), G_hi[:, j, :].bitcast(F32),
                                  ALU.subtract).then_inc(G_lo_ready, 1)

            def low_parts(half, first, end):
                with dve.Fori(first, end) as i:
                    for j in range(4):
                        low_part(half, i, j)

            overlapped_base = steps[0]

            def overlapped(i, q, is_last=False):
                before = one(i + (TILES // 2 + q)), 1 - q
                following = one(i + (TILES // 2 + 1 + q)), 1 - q
                multiply(*before, i * 2 + (half_tile + 1 + q))
                low_part(0, i * 2 + (q + 1), 0)
                if not is_last:
                    onehots_xy(*following)
                low_part(0, i * 2 + (q + 1), 1)
                if not is_last:
                    weigh_x(*following, i * 2 + (overlapped_base + q + 1))
                low_part(0, i * 2 + (q + 1), 2)
                low_part(0, i * 2 + (q + 1), 3)

            low_parts(0, 0, 1)
            with dve.Fori(0, OVERLAPPED // 2 - 1) as i:
                for q in range(2):
                    overlapped(i, q)
            for q in range(2):
                overlapped(OVERLAPPED // 2 - 1, q, is_last=(q == 1))
            steps[0] += OVERLAPPED - 1
            multiply(one(TILES - 1), 1, HALF_TILES - 1)
            low_parts(0, OVERLAPPED + 1, TILES)

            def statistics(*tiles):
                for t in tiles:
                    dve.wait_ge(out_turned, t + 1)
                    if t >= 4:
                        dve.wait_ge(stored[t % 4], 16)
                    dve.tensor_tensor(result[:, t % 4, :], out_slot(t), h1[:, t, :], ALU.add).then_inc(dve_step, 1)
                for n, t in enumerate(tiles):
                    dve.wait_ge(dve_step, steps[0] + n + 1)
                    dve.bn_stats(stat(t % 4, STATS, 6), result[:, t % 4, :]).then_inc(dve_step, 1)
                for n, t in enumerate(tiles):
                    dve.wait_ge(dve_step, steps[0] + len(tiles) + n + 1)
                    dve.bn_aggr(stat(t % 4, MEAN, 2), stat(t % 4, STATS, 6)).then_inc(dve_step, 1)
                steps[0] += 3 * len(tiles)
                dve.wait_ge(dve_step, steps[0])
                dve.tensor_scalar(stats_of(tiles, VAR_EPS), stats_of(tiles, VAR), EPS, None, ALU.add
                                  ).then_inc(var2_ready, len(tiles))

            def normalise(t):
                y2 = result[:, t % 4, :]
                dve.wait_ge(rstd2_ready, t + 1)
                dve.tensor_scalar(y2, y2, stat(t % 4, MEAN), stat(t % 4, RSTD),
                                  ALU.subtract, ALU.mult).then_inc(result_ready, 1)

            for t in range(TILES // 2):
                low_parts(1, TILES + 2 * t, TILES + 2 * t + 2)
                statistics(t)
                if t > 0:
                    normalise(t - 1)
            dve.wait_ge(G_free, 4 + 2 * CHUNKS)
            dve.tensor_scalar(outT[:, DK - 1, :], sums[1][DK - 1], 1.0 / WSCALE, None, ALU.mult
                              ).then_inc(outT_by_dve, 1)
            normalise(TILES // 2 - 1)
            for tiles in LATE_TILES[TILES // 2:]:
                statistics(*tiles)
            for t in range(TILES // 2, TILES):
                normalise(t)


_ARGS = ["x", "L0_tok_W", "L0_tok_b", "L0_tok_pos_emb", "L0_attn_W", "L0_ffn_w_queries", "L0_ffn_keys",
         "L0_ffn_down_embed", "L0_ffn_up_embed", "L0_ffn_w_gate", "L0_ffn_w_up", "L0_ffn_w_down"]


def constant_tables():
    import numpy as np

    row = np.arange(P)
    image, patch = row // PATCHES, row % PATCHES
    seen = (image[:, None] == image[None, :]) & (patch[None, :] <= patch[:, None])
    quadrant = row // 32
    return np.concatenate([np.eye(P), np.where(seen, 0.0, -3e38),
                           quadrant[:, None] % 2 == np.arange(2)[None, :]], axis=1).astype(np.float32)


def kernel(**inputs):
    import numpy as np
    import concourse.bacc as bacc
    from concourse.bass_utils import run_bass_kernel_spmd

    nc = bacc.Bacc("TRN2", target_bir_lowering=False, num_devices=1)
    arrays, args = {}, []
    named = [(name, np.ascontiguousarray(inputs[name])) for name in _ARGS] + [("constants", constant_tables())]
    for name, a in named:
        arrays[f"in_{name}"] = a
        args.append(nc.dram_tensor(f"in_{name}", a.shape, mybir.dt.from_np(a.dtype), kind="ExternalInput").ap())
    out = nc.dram_tensor("out_h", (IMAGES, PATCHES, D), F32, kind="ExternalOutput").ap()
    vit_block_kernel(nc, *args, out)
    run = run_bass_kernel_spmd(nc, [arrays], core_ids=[0])
    return run.results[0]["out_h"]
```
